# Optimizing a Trainium2 kernel written in Bass

```python
import numpy as np
import jax
import jax.numpy as jnp

def _softmax(x, axis=-1):
    return jax.nn.softmax(x, axis=axis)

def _gelu(x):
    return jax.nn.gelu(x, approximate=True)

def _silu(x):
    return jax.nn.silu(x)

def _sigmoid(x):
    return jax.nn.sigmoid(x)

def _layernorm(x, axis=-1, eps=1e-05):
    m = jnp.mean(x, axis=axis, keepdims=True)
    v = jnp.var(x, axis=axis, keepdims=True)
    return (x - m) / jnp.sqrt(v + eps)

def _scatter_add(tgt, idx, src, axis=0):
    return tgt.at[idx].add(src)

def _segment_sum(src, seg, n):
    return jax.ops.segment_sum(src, seg, n)
kernel_name = 'mk_seq_preln_d1_jaxref_r8_322291'

def setup_inputs(seed: int=0):
    np.random.seed(seed)
    _w = jnp.asarray

    def _L0_attn_setup():
        import jax, jax.numpy as jnp
        import numpy as np
        D_MODEL = 128
        NUM_HEADS = 16
        D_K = D_MODEL // NUM_HEADS
        MAX_LEN = 128
        BATCH = 8
        SEQ = 128
        key = jax.random.key(seed)
        ks = jax.random.split(key, 12)
        s = 0.02
        inp = {'x': jax.random.normal(ks[0], (BATCH, SEQ, D_MODEL), dtype=jnp.float32), 'Wq': jax.random.normal(ks[1], (D_MODEL, D_MODEL), dtype=jnp.float32) * s, 'bq': jnp.zeros((D_MODEL,), dtype=jnp.float32), 'Wk': jax.random.normal(ks[2], (D_MODEL, D_MODEL), dtype=jnp.float32) * s, 'bk': jnp.zeros((D_MODEL,), dtype=jnp.float32), 'Wv': jax.random.normal(ks[3], (D_MODEL, D_MODEL), dtype=jnp.float32) * s, 'bv': jnp.zeros((D_MODEL,), dtype=jnp.float32), 'Wo': jax.random.normal(ks[4], (D_MODEL, D_MODEL), dtype=jnp.float32) * s, 'bo': jnp.zeros((D_MODEL,), dtype=jnp.float32), 'relative_k': jax.random.normal(ks[5], (2 * MAX_LEN - 1, D_K), dtype=jnp.float32), 'relative_v': jax.random.normal(ks[6], (2 * MAX_LEN - 1, D_K), dtype=jnp.float32)}
        return inp
    _L0_attn_in = _L0_attn_setup()

    def _L0_ffn_setup():
        import jax, jax.numpy as jnp
        import numpy as np
        TOP_K = 2

        def gelu(x):
            return jax.nn.gelu(x, approximate=False)
        key = jax.random.key(seed)
        ks = jax.random.split(key, 6)
        B, L, D, H, E, S = (4, 256, 128, 256, 8, 2)
        sd = 0.02
        return {'x': jax.random.normal(ks[0], (B, L, D), dtype=jnp.float32), 'router_w': jax.random.normal(ks[1], (D, E), dtype=jnp.float32) * sd, 'router_b': jnp.zeros((E,), dtype=jnp.float32), 'w1': jax.random.normal(ks[2], (E, D, H), dtype=jnp.float32) * sd, 'b1': jnp.zeros((E, H), dtype=jnp.float32), 'w2': jax.random.normal(ks[3], (E, H, D), dtype=jnp.float32) * sd, 'b2': jnp.zeros((E, D), dtype=jnp.float32), 'sw1': jax.random.normal(ks[4], (S, D, H), dtype=jnp.float32) * sd, 'sb1': jnp.zeros((S, H), dtype=jnp.float32), 'sw2': jax.random.normal(ks[5], (S, H, D), dtype=jnp.float32) * sd, 'sb2': jnp.zeros((S, D), dtype=jnp.float32)}
    _L0_ffn_in = _L0_ffn_setup()
    _d = {'L0_attn_x': _L0_attn_in['x'], 'L0_attn_Wq': _L0_attn_in['Wq'], 'L0_attn_bq': _L0_attn_in['bq'], 'L0_attn_Wk': _L0_attn_in['Wk'], 'L0_attn_bk': _L0_attn_in['bk'], 'L0_attn_Wv': _L0_attn_in['Wv'], 'L0_attn_bv': _L0_attn_in['bv'], 'L0_attn_Wo': _L0_attn_in['Wo'], 'L0_attn_bo': _L0_attn_in['bo'], 'L0_attn_relative_k': _L0_attn_in['relative_k'], 'L0_attn_relative_v': _L0_attn_in['relative_v'], 'L0_ffn_router_w': _L0_ffn_in['router_w'], 'L0_ffn_router_b': _L0_ffn_in['router_b'], 'L0_ffn_w1': _L0_ffn_in['w1'], 'L0_ffn_b1': _L0_ffn_in['b1'], 'L0_ffn_w2': _L0_ffn_in['w2'], 'L0_ffn_b2': _L0_ffn_in['b2'], 'L0_ffn_sw1': _L0_ffn_in['sw1'], 'L0_ffn_sb1': _L0_ffn_in['sb1'], 'L0_ffn_sw2': _L0_ffn_in['sw2'], 'L0_ffn_sb2': _L0_ffn_in['sb2']}
    _x0 = _d['L0_attn_x']
    _d['L0_attn_x'] = jax.random.normal(jax.random.fold_in(jax.random.key(seed), 1), (16, 512, 128), dtype=_x0.dtype)
    del _x0
    return _d

def reference(L0_attn_x, L0_attn_Wq, L0_attn_bq, L0_attn_Wk, L0_attn_bk, L0_attn_Wv, L0_attn_bv, L0_attn_Wo, L0_attn_bo, L0_attn_relative_k, L0_attn_relative_v, L0_ffn_router_w, L0_ffn_router_b, L0_ffn_w1, L0_ffn_b1, L0_ffn_w2, L0_ffn_b2, L0_ffn_sw1, L0_ffn_sb1, L0_ffn_sw2, L0_ffn_sb2):

    def _L0_attn_ref(x, Wq, bq, Wk, bk, Wv, bv, Wo, bo, relative_k, relative_v):
        import jax, jax.numpy as jnp
        import numpy as np
        D_MODEL = 128
        NUM_HEADS = 16
        D_K = D_MODEL // NUM_HEADS
        MAX_LEN = 128
        BATCH = 8
        SEQ = 128
        B, L, D = x.shape
        H, dk = (NUM_HEADS, D_K)
        Q = (x @ Wq.T + bq).reshape(B, L, H, dk).transpose(0, 2, 1, 3)
        K = (x @ Wk.T + bk).reshape(B, L, H, dk).transpose(0, 2, 1, 3)
        V = (x @ Wv.T + bv).reshape(B, L, H, dk).transpose(0, 2, 1, 3)
        rel_pos = jnp.arange(L)[None, :] - jnp.arange(L)[:, None] + (MAX_LEN - 1)
        rel_k = relative_k[rel_pos]
        rel_v = relative_v[rel_pos]
        scale = 1.0 / np.sqrt(dk).astype(np.float32)
        scores = jnp.einsum('bhld,bhrd->bhlr', Q, K) * scale
        scores = scores + jnp.einsum('bhld,lrd->bhlr', Q, rel_k)
        attn = jax.nn.softmax(scores, axis=-1)
        out = jnp.einsum('bhlr,bhrd->bhld', attn, V)
        out = out + jnp.einsum('bhlr,lrd->bhld', attn, rel_v)
        out = out.transpose(0, 2, 1, 3).reshape(B, L, D)
        return out @ Wo.T + bo

    def _L0_ffn_ref(x, router_w, router_b, w1, b1, w2, b2, sw1, sb1, sw2, sb2):
        import jax, jax.numpy as jnp
        import numpy as np
        TOP_K = 2

        def gelu(x):
            return jax.nn.gelu(x, approximate=False)
        B, L, D = x.shape
        E = router_b.shape[0]
        S = sw1.shape[0]
        xf = x.reshape(-1, D)
        sh = gelu(jnp.einsum('nd,sdh->snh', xf, sw1) + sb1[:, None, :])
        shared_out = (jnp.einsum('snh,shd->nd', sh, sw2) + sb2.sum(0)) / S
        gates = xf @ router_w + router_b
        topv, topi = jax.lax.top_k(gates, TOP_K)
        probs = jax.nn.softmax(topv, axis=-1)
        comb = jnp.einsum('nke,nk->ne', jax.nn.one_hot(topi, E, dtype=xf.dtype), probs)
        h = gelu(jnp.einsum('nd,edh->enh', xf, w1) + b1[:, None, :])
        y = jnp.einsum('enh,ehd->end', h, w2) + b2[:, None, :]
        moe_out = jnp.einsum('ne,end->nd', comb, y)
        return (shared_out + moe_out).reshape(B, L, D)
    x = L0_attn_x
    x = x + _L0_attn_ref(_layernorm(x, axis=-1), L0_attn_Wq, L0_attn_bq, L0_attn_Wk, L0_attn_bk, L0_attn_Wv, L0_attn_bv, L0_attn_Wo, L0_attn_bo, L0_attn_relative_k, L0_attn_relative_v)
    x = x + _L0_ffn_ref(_layernorm(x, axis=-1), L0_ffn_router_w, L0_ffn_router_b, L0_ffn_w1, L0_ffn_b1, L0_ffn_w2, L0_ffn_b2, L0_ffn_sw1, L0_ffn_sb1, L0_ffn_sw2, L0_ffn_sb2)
    return x

_drawn_inputs = setup_inputs


def setup_inputs(seed=0):
    import zlib

    import numpy as np

    out = dict(_drawn_inputs(seed))
    spreads = {'L0_attn_bq': (0.0, 0.703),
     'L0_attn_bk': (0.0, 0.8),
     'L0_attn_bv': (0.0, 0.358),
     'L0_attn_bo': (0.0, 0.1),
     'L0_ffn_router_b': (0.0, 0.1),
     'L0_ffn_b1': (0.0, 0.688),
     'L0_ffn_b2': (0.0, 0.1),
     'L0_ffn_sb1': (0.0, 0.689),
     'L0_ffn_sb2': (0.0, 0.1)}
    factors = {'L0_attn_Wk': 8.0, 'L0_attn_Wv': 8.0}
    for name, (base, spread) in spreads.items():
        noise = np.random.default_rng([zlib.crc32(name.encode()), seed]).standard_normal(out[name].shape)
        drawn = base * np.exp(spread * noise) if base else spread * noise
        out[name] = jnp.asarray(drawn.astype(out[name].dtype))
    for name, factor in factors.items():
        out[name] = (out[name] * factor).astype(out[name].dtype)
    return out
```

```python
import math
from contextlib import ExitStack

import numpy as np

import concourse.bass as bass
from concourse import mybir

F32 = mybir.dt.float32
F16 = mybir.dt.float16
U32 = mybir.dt.uint32
U8 = mybir.dt.uint8
ALU = mybir.AluOpType
ACT = mybir.ActivationFunctionType
AX_X = mybir.AxisListType.X

P = 128
B, L, D = 16, 512, 128
H, DK = 16, 8
MAX_LEN = 128
NE, NS, HID = 8, 2, 256
EXPERTS = NS + NE
LN_EPS = 1e-5
SCALE = float(np.float32(1.0) / np.sqrt(DK).astype(np.float32))

PAIRS = B // 2
TOK = 2 * L
QT = 4
QUADS = 8
ROWS = QT * QUADS
STEPS = L // ROWS
RT = L // P
TILES = STEPS * QUADS
REL_K = 3 * QT * DK
WIN = L + ROWS - QT
RK_COLS = 2 * L - QT
RV_COLS = (L - ROWS) + L
NT = B * L // P
TPB = L // P
S_BANKS = 4
START = 1
LAG = 2
ACT_EVAC = (0, 1, 2, 4, 5, 6)
DVE_EVAC = (3, 7)
M4, M16, IOTA = 0, 4, 20
IDENT = 28
CONSTS = IDENT + P


def attention_ffn(nc, x, wq_t, wk_t, wv_t, wo_t, bq, bk, bv, bo, rk_win, rv_win, rw, rb, w1, w2, b2,
                  sw1, sw2, sb2, b1_cols, consts, rel_scratch, out):
    with ExitStack() as ctx:
        def sb(name, shape, dt=F32):
            return ctx.enter_context(nc.sbuf_tensor(name, shape, dt))

        def sem(name):
            return ctx.enter_context(nc.semaphore(name))

        ps = ctx.enter_context(nc.psum_tensor("ps", [P, 8, 512], F32))

        x_all = sb("x_all", [P, NT, D])
        attn_t = sb("attn_t", [P, B * L])
        const = sb("const", [P, CONSTS])
        m4, iota8, ident = const[:, M4:M4 + 4], const[:, IOTA:IOTA + NE], const[:, IDENT:IDENT + P]
        mask16h = sb("mask16h", [P, H], F16)
        mask4h = sb("mask4h", [P, QT, DK], F16)
        identh = sb("identh", [P, P], F16)
        wq_s, wk_s, wv_s, wo_s = (sb(n, [P, D]) for n in ("wq_s", "wk_s", "wv_s", "wo_s"))
        bq_col, bk_col, bks_col = (sb(n, [P, 1]) for n in ("bq_col", "bk_col", "bks_col"))
        bq_row, bv_row, bo_row = (sb(n, [P, D]) for n in ("bq_row", "bv_row", "bo_row"))
        rk3 = sb("rk3", [REL_K, RK_COLS])
        rk_split = sb("rk_split", [REL_K, RK_COLS], F16)
        rw_s = sb("rw_s", [P, NE])
        rb_row = sb("rb_row", [P, NE])
        w1_s = sb("w1_s", [P, EXPERTS, HID])
        w2_s = sb("w2_s", [P, EXPERTS, 2, D])
        b1_s = sb("b1_s", [P, EXPERTS, 2])
        b2_s = sb("b2_s", [EXPERTS, D])
        half_pow = sb("half_pow", [P, 8])
        e_const = sb("e_const", [P, TPB])

        settled = sb("settled", [P, 1])
        stats = sb("stats", [P, 8, 6])
        mv = sb("mv", [P, 8, 2])
        var_eps = sb("var_eps", [P, 8])
        rstd = sb("rstd", [P, 8])
        xn = sb("xn", [P, 8, D])
        xn_t = sb("xn_t", [P, TOK])
        q_hi, q_lo, k_hi, k_lo = (sb(n, [P, TOK], F16) for n in ("q_hi", "q_lo", "k_hi", "k_lo"))
        v_s = sb("v_s", [P, 8, D])
        q_nat = sb("q_nat", [P, 2, QT, D])
        q_split = sb("q_split", [P, 2, H, 3, QT, DK], F16)
        q_rel = sb("q_rel", [REL_K, P, 4, DK], F16)

        stat_hi = sb("stat_hi", [P, 2, QUADS, 2, ROWS], F16)
        stat_lo = sb("stat_lo", [P, 2, QUADS, 2, ROWS], F16)
        stat_rel = sb("stat_rel", [REL_K, QUADS, 4, QT, DK], F16)
        rk_step = sb("rk_step", [REL_K, WIN], F16)
        rv_step = sb("rv_step", [P, RT, ROWS * DK])
        neg_max = sb("neg_max", [P, QUADS])
        row_sum = sb("row_sum", [P, QUADS])
        inv_sum = sb("inv_sum", [P, QUADS])
        probs = sb("probs", [P, QUADS, L])
        probs_t = sb("probs_t", [P, QUADS, RT, P])
        v_masked = sb("v_masked", [P, 2 * ROWS, 4])
        r_masked = sb("r_masked", [P, 8, QT, DK])
        rel_o = sb("rel_o", [P, 2, 32])
        rel_t = sb("rel_t", [32, STEPS, 2, P])

        rel_nat = v_s[:, 0:TPB, :].rearrange("p t (h d) -> p t h d", h=H)
        o_sum_t = xn_t[:, 0:L]
        h_t = q_nat[:].rearrange("p b l c -> p b (l c)")
        gates = sb("gates", [P, TPB, NE])
        top8 = sb("top8", [P, TPB, 8])
        top_i = sb("top_i", [P, TPB, 8], U32)
        top_f = sb("top_f", [P, TPB, 2])
        gap = sb("gap", [P, TPB])
        e_gap = sb("e_gap", [P, TPB])
        prob2 = sb("prob2", [P, TPB, 2])
        pick = sb("pick", [P, TPB, 2, NE])
        comb = sb("comb", [P, 2, TPB, EXPERTS])
        comb_t = sb("comb_t", [EXPERTS, L])
        acc = sb("acc", [P, 2, TPB, D])
        hid = probs[:, 0:4, :].rearrange("p (e k) c -> p e k c", e=2)

        loaded = sem("loaded")
        setup_dve = sem("setup_dve")
        setup_pool = sem("setup_pool")
        var_ready, rstd_ready, xn_ready, xn_tr = sem("var_ready"), sem("rstd_ready"), sem("xn_ready"), sem("xn_tr")
        xn_t_ready, proj_done, hi_ready = sem("xn_t_ready"), sem("proj_done"), sem("hi_ready")
        dve_link = sem("dve_link")
        operands_ready, q_split_ready, q_rel_tr = sem("operands_ready"), sem("q_split_ready"), sem("q_rel_tr")
        q_rel_ready = sem("q_rel_ready")
        stat_ready, stat_rel_ready = sem("stat_ready"), sem("stat_rel_ready")
        rk_landed, rv_landed = sem("rk_landed"), sem("rv_landed")
        score_done, max_done, exp_done, inv_done = sem("score_done"), sem("max_done"), sem("exp_done"), sem("inv_done")
        norm_done, tr_done, evac_act, evac_dve = sem("norm_done"), sem("tr_done"), sem("evac_act"), sem("evac_dve")
        av_v_done, av_r_done, v_red, r_red = sem("av_v_done"), sem("av_r_done"), sem("v_red"), sem("r_red")
        step_link = sem("step_link")
        rel_tr, rel_t_ready, rel_stored = sem("rel_tr"), sem("rel_t_ready"), sem("rel_stored")
        rel_landed, rel_nat_tr, o_ready, wo_done = sem("rel_landed"), sem("rel_nat_tr"), sem("o_ready"), sem("wo_done")
        ffn_link, x1_var, x1_rstd = sem("ffn_link"), sem("x1_var"), sem("x1_rstd")
        hn_ready, hn_tr, h_ready = sem("hn_ready"), sem("hn_tr"), sem("h_ready")
        gate_done, gap_ready, e_gap_ready, comb_ready = sem("gate_done"), sem("gap_ready"), sem("e_gap_ready"), sem("comb_ready")
        comb_tr, comb_t_ready, bias_done, acc_ready = sem("comb_tr"), sem("comb_t_ready"), sem("bias_done"), sem("acc_ready")
        up_done, gelu_done, down_done, y_used = sem("up_done"), sem("gelu_done"), sem("down_done"), sem("y_used")
        final_ready, stored = sem("final_ready"), sem("stored")

        LOADS = 26
        SETUP_DVE = 7
        SETUP_POOL = 3

        counted = (av_r_done, av_v_done, bias_done, comb_ready, comb_t_ready, comb_tr, down_done, dve_link,
                   e_gap_ready, evac_act, evac_dve, exp_done, ffn_link, final_ready, gap_ready, gate_done,
                   gelu_done, h_ready, hi_ready, hn_ready, hn_tr, inv_done, max_done, norm_done,
                   o_ready, operands_ready, proj_done, q_rel_ready, q_rel_tr, q_split_ready, r_red, rel_landed,
                   rel_nat_tr, rel_stored, rel_t_ready, rel_tr, rk_landed, rstd_ready, rv_landed, score_done,
                   stat_ready, stat_rel_ready, step_link, stored, tr_done, up_done, v_red, var_ready,
                   wo_done, x1_rstd, x1_var, xn_ready, xn_t_ready, xn_tr, y_used)

        block = ctx.enter_context(nc.Block())

        def bank_h(bank, n):
            return ps[:, bank, :].bitcast(F16)[:, 0:n]

        @block.sync
        def _(sp):
            for semaphore in counted:
                sp.sem_inc(semaphore, START)

            def load(dst, src):
                sp.dma_start(dst, src).then_inc(loaded, 16)

            load(x_all[:, 0:NT // 2, :], x[0:B * L // 2, :].rearrange("(t p) d -> p t d", p=P))
            load(x_all[:, NT // 2:NT, :], x[B * L // 2:B * L, :].rearrange("(t p) d -> p t d", p=P))
            load(const[:], consts)
            for dst, src in ((wq_s, wq_t), (wk_s, wk_t), (wv_s, wv_t), (wo_s, wo_t)):
                load(dst[:], src)
            for dst, src in ((bq_col, bq), (bk_col, bk)):
                load(dst[:], src.rearrange("(p a) -> p a", a=1))
            for dst, src in ((bq_row, bq), (bv_row, bv), (bo_row, bo), (rb_row, rb)):
                load(dst[:], src.partition_broadcast(P))
            for piece in range(3):
                load(rk3[piece * 32:piece * 32 + 32, :], rk_win)
            load(rw_s[:], rw)
            load(w1_s[:, 0:NS, :], sw1.rearrange("e d h -> d e h"))
            load(w1_s[:, NS:, :], w1.rearrange("e d h -> d e h"))
            for k in range(2):
                load(w2_s[:, 0:NS, k, :], sw2[:, k * P:(k + 1) * P, :].rearrange("e h d -> h e d"))
                load(w2_s[:, NS:, k, :], w2[:, k * P:(k + 1) * P, :].rearrange("e h d -> h e d"))
            load(b1_s[:], b1_cols)
            load(b2_s[0:NS, :], sb2)
            load(b2_s[NS:, :], b2)

            def value_window(s, multiplied):
                at = sp.snap(sp.to_reg(ROWS * DK * 4 * s))
                blocks = rv_win.bitcast(U8)[:, bass.ds(at, RT * P * DK * 4)].rearrange("p (t c) -> p t c", t=RT)
                sp.wait_ge(av_r_done, START + multiplied)
                sp.dma_start(rv_step[:].bitcast(U8), blocks[:, :, 0:ROWS * DK * 4]).then_inc(rv_landed, 16)

            with sp.Fori(0, PAIRS) as pair:
                with sp.Fori(0, STEPS) as s:
                    value_window(s, pair * STEPS + s)
                row = sp.snap(sp.to_reg(pair * 32))
                sp.wait_ge(rel_t_ready, START + (pair + 1) * STEPS)
                sp.dma_start(rel_scratch[bass.ds(row, 32), :], rel_t[:].rearrange("p s a c -> p (s a c)")).then_inc(rel_stored, 16)
            sp.wait_ge(rel_stored, START + PAIRS * 16)

            rel_rows = rel_scratch.rearrange("(b h) (t p d) -> b t p h d", h=H, p=P, d=DK)

            def load_rel(b):
                for t in range(TPB):
                    sp.dma_start(rel_nat[:, t, :, :], rel_rows[bass.ds(b, 1), t, :, :, :].rearrange("b p h d -> (b p) h d")).then_inc(rel_landed, 16)

            load_rel(0)
            out_rows = out.rearrange("(b t p) d -> b p t d", t=TPB, p=P)

            def store(b, slot):
                b = sp.snap(sp.to_reg(b))
                sp.wait_ge(final_ready, START + b + 1)
                sp.dma_start(out_rows[bass.ds(b, 1), :, :, :].rearrange("b p t d -> (b p) t d"), acc[:, slot, :, :]).then_inc(stored, 16)

            with sp.Fori(0, B // 2 - 1) as i:
                for slot in range(2):
                    following = sp.snap(sp.to_reg(2 * i + slot + 1))
                    sp.wait_ge(rel_nat_tr, START + following)
                    load_rel(following)
                    store(2 * i + slot, slot)
            sp.wait_ge(rel_nat_tr, START + B - 1)
            load_rel(B - 1)
            store(B - 2, 0)
            store(B - 1, 1)
            sp.wait_ge(stored, START + 16 * B)

        @block.gpsimd
        def _(pool):
            nc.gpsimd.memset(half_pow[:], -0.5).then_inc(setup_pool, 1)
            nc.gpsimd.memset(e_const[:], math.e).then_inc(setup_pool, 1)
            nc.gpsimd.memset(comb[:], 1.0 / NS).then_inc(setup_pool, 1)
            pool.wait_ge(setup_pool, SETUP_POOL)
            pool.wait_ge(setup_dve, SETUP_DVE)

            def relative_queries(s):
                quads = q_rel[:, bass.ds(s * QUADS, QUADS), :, :].rearrange("k q g h -> k (q g) h")
                nc.gpsimd.tensor_tensor(
                    stat_rel[:].rearrange("k q g l h -> k (q g) l h"),
                    quads.unsqueeze(2).broadcast_to([REL_K, QUADS * 4, QT, DK]),
                    mask4h[0:REL_K].unsqueeze(1).broadcast_to([REL_K, QUADS * 4, QT, DK]), ALU.mult).then_inc(stat_rel_ready, 1)

            def normalise(done, q):
                pool.wait_ge(inv_done, START + done + q + 1)
                nc.gpsimd.tensor_tensor(probs[:, q, :], probs[:, q, :], inv_sum[:, q:q + 1].broadcast_to([P, L]),
                                        ALU.mult).then_inc(norm_done, 1)

            with pool.Fori(0, PAIRS) as pair:
                pool.wait_ge(var_ready, START + pair + 1)
                nc.gpsimd.tensor_tensor(rstd[:], var_eps[:], half_pow[:], ALU.pow).then_inc(rstd_ready, 1)
                pool.wait_ge(q_rel_ready, START + (pair + 1) * 4)
                relative_queries(0)
                with pool.Fori(0, STEPS - 1) as s:
                    for q in range(QUADS):
                        if q == 6:
                            pool.wait_ge(score_done, START + pair * TILES + (s + 1) * QUADS)
                            relative_queries(s + 1)
                        normalise(pair * TILES + s * QUADS, q)
                for q in range(QUADS):
                    normalise(pair * TILES + (STEPS - 1) * QUADS, q)

            def prepare(b):
                pool.wait_ge(x1_var, START + b + 1)
                nc.gpsimd.tensor_tensor(rstd[:, 0:TPB], var_eps[:, 0:TPB], half_pow[:, 0:TPB], ALU.pow).then_inc(x1_rstd, 1)
                pool.wait_ge(gap_ready, START + b + 1)
                nc.gpsimd.tensor_tensor(e_gap[:], e_const[:], gap[:], ALU.pow).then_inc(e_gap_ready, 1)

            with pool.Fori(0, B) as b:
                prepare(b)

        @block.scalar
        def _(act):
            act.wait_ge(loaded, 16 * LOADS)
            act.wait_ge(setup_dve, SETUP_DVE)

            def prepare(pair):
                for half in range(2):
                    act.wait_ge(xn_tr, START + pair * 2 + half + 1)
                    nc.scalar.activation(xn_t[:, half * L:(half + 1) * L], ps[:, half, :], ACT.Copy).then_inc(xn_t_ready, 1)
                for n, (hi, bias) in enumerate(((q_hi, bq_col), (q_hi, bq_col), (k_hi, bks_col), (k_hi, bks_col))):
                    act.wait_ge(proj_done, START + pair * 8 + n + 1)
                    nc.scalar.activation(hi[:, (n % 2) * L:(n % 2 + 1) * L], ps[:, 2 + n, :], ACT.Identity,
                                         bias=bias[:, 0:1]).then_inc(hi_ready, 1)
                for n in range(4):
                    act.wait_ge(q_rel_tr, START + pair * 4 + n + 1)
                    nc.scalar.activation(q_rel[:, :, n, :], bank_h(2 + n, 8 * P)[0:REL_K, :].rearrange("k (h q) -> k q h", h=DK),
                                         ACT.Copy).then_inc(q_rel_ready, 1)

            def key_window(pair, s):
                act.wait_ge(score_done, START + pair * TILES + s * QUADS)
                act.dma_start(rk_step[:], rk_split[:, bass.ds(L - ROWS - ROWS * s, WIN)]).then_inc(rk_landed, 16)

            def evacuate(pair, s, q):
                act.wait_ge(tr_done, START + pair * TILES + s * QUADS + q + 1)
                nc.scalar.activation(probs_t[:, q, :, :].rearrange("p r c -> p (r c)"), ps[:, 4 + q % 2, :], ACT.Copy).then_inc(evac_act, 1)

            def exponentials(pair, s, q, first):
                act.wait_ge(max_done, START + pair * TILES + s * QUADS + q + 1)
                if not first:
                    act.wait_ge(tr_done, START + pair * TILES + (s - 1) * QUADS + q + 1)
                nc.scalar.activation(probs[:, q, :], ps[:, q % S_BANKS, :], ACT.Exp, bias=neg_max[:, q:q + 1],
                                     accum_out=row_sum[:, q:q + 1]).then_inc(exp_done, 1)

            def rel_out(pair, s):
                act.wait_ge(rel_tr, START + pair * STEPS + s + 1)
                nc.scalar.activation(rel_t[:, bass.ds(s, 1), :, :].rearrange("p s a c -> p (s a c)"), ps[0:32, 6, 256:512],
                                     ACT.Copy).then_inc(rel_t_ready, 1)

            def step(pair, s, first=False, rel=True, last=False, more=True):
                for q in range(QUADS):
                    if not first and q in ACT_EVAC:
                        evacuate(pair, s - 1, q)
                    if rel and q == 5:
                        rel_out(pair, s - 2)
                    if not last and q:
                        exponentials(pair, s, q - 1, first)
                if not last:
                    exponentials(pair, s, QUADS - 1, first)
                    if more:
                        key_window(pair, s + 1)

            with act.Fori(0, PAIRS) as pair:
                key_window(pair, 0)
                prepare(pair)
                step(pair, 0, first=True, rel=False)
                act.wait_ge(rel_stored, START + pair * 16)
                step(pair, 1, rel=False)
                with act.Fori(2, STEPS - 1) as s:
                    step(pair, s)
                step(pair, STEPS - 1, more=False)
                step(pair, STEPS, last=True)
                rel_out(pair, STEPS - 1)

            def prepare_h(b, slot):
                act.wait_ge(hn_tr, START + b + 1)
                nc.scalar.activation(h_t[:, slot, :], ps[:, 0, :], ACT.Copy).then_inc(h_ready, 1)

            def batch(b, slot, ahead):
                for e in range(EXPERTS):
                    for k in range(2):
                        act.wait_ge(up_done, START + b * 20 + e * 2 + k + 1)
                        act.wait_ge(down_done, START + b * EXPERTS + max(e - 1, 0))
                        nc.scalar.activation(hid[:, e % 2, k, :], ps[:, 4 + k, :], ACT.Gelu, bias=b1_s[:, e, k:k + 1]).then_inc(gelu_done, 1)
                    if ahead and e == 5:
                        prepare_h(b + 1, 1 - slot)
                    if ahead and e == 8:
                        prepare_weights(b + 1)

            def prepare_weights(b):
                act.wait_ge(comb_tr, START + b + 1)
                nc.scalar.activation(comb_t[:], ps[0:EXPERTS, 1, :], ACT.Copy).then_inc(comb_t_ready, 1)

            prepare_h(0, 0)
            prepare_weights(0)
            with act.Fori(0, B // 2 - 1) as i:
                batch(2 * i, 0, True)
                batch(2 * i + 1, 1, True)
            batch(B - 2, 0, True)
            batch(B - 1, 1, False)

        @block.vector
        def _(dve):
            dve.wait_ge(loaded, 16 * LOADS)
            nc.vector.tensor_copy(mask16h[:], const[:, M16:M16 + H]).then_inc(setup_dve, 1)
            nc.vector.tensor_copy(mask4h[:], m4.unsqueeze(2).broadcast_to([P, QT, DK])).then_inc(setup_dve, 1)
            nc.vector.tensor_copy(identh[:], ident).then_inc(setup_dve, 1)
            nc.vector.tensor_copy(rk_split[:], rk3[:]).then_inc(setup_dve, 1)
            nc.vector.tensor_scalar(wk_s[:], wk_s[:], SCALE, None, ALU.mult).then_inc(setup_dve, 1)
            nc.vector.tensor_scalar(bks_col[:], bk_col[:], SCALE, None, ALU.mult).then_inc(setup_dve, 1)
            dve.wait_ge(setup_dve, 6)
            nc.vector.tensor_tensor(rk_split[32:64, :], rk3[32:64, :], rk_split[32:64, :], ALU.subtract).then_inc(setup_dve, 1)
            dve.wait_ge(setup_dve, SETUP_DVE)
            dve.wait_ge(setup_pool, SETUP_POOL)

            class Links:
                def __init__(self, semaphore, before):
                    self.semaphore, self.before, self.n = semaphore, before, 0

                def __call__(self, ins):
                    self.n += 1
                    ins.then_inc(self.semaphore, 1)

                def wait(self):
                    dve.wait_ge(self.semaphore, START + self.before + self.n)

                def settle(self):
                    self.wait()
                    nc.vector.memset(settled[:], 0.0)

            PREP_LINKS = 13

            def prepare(pair):
                link = Links(dve_link, pair * PREP_LINKS)
                for t in range(8):
                    link(nc.vector.bn_stats(stats[:, t, :], x_all[:, bass.ds(pair * 8 + t, 1), :].rearrange("p a d -> p (a d)")))
                link.settle()
                for t in range(8):
                    last = nc.vector.bn_aggr(mv[:, t, :], stats[:, t, :])
                link(last)
                link.wait()
                nc.vector.tensor_scalar(var_eps[:], mv[:, :, 1], LN_EPS, None, ALU.add).then_inc(var_ready, 1)
                dve.wait_ge(rstd_ready, START + pair + 1)
                for t in range(8):
                    nc.vector.tensor_scalar(xn[:, t, :], x_all[:, bass.ds(pair * 8 + t, 1), :].rearrange("p a d -> p (a d)"),
                                            mv[:, t, 0:1], rstd[:, t:t + 1], ALU.subtract, ALU.mult).then_inc(xn_ready, 1)
                for n, (hi, lo, bias) in enumerate(((q_hi, q_lo, bq_col), (q_hi, q_lo, bq_col), (k_hi, k_lo, bks_col), (k_hi, k_lo, bks_col))):
                    dve.wait_ge(hi_ready, START + pair * 4 + n + 1)
                    cols = slice((n % 2) * L, (n % 2 + 1) * L)
                    nc.vector.scalar_tensor_tensor(lo[:, cols], ps[:, 2 + n, :], bias[:, 0:1], hi[:, cols], ALU.add,
                                                   ALU.subtract).then_inc(operands_ready, 1)
                for b in range(2):
                    dve.wait_ge(proj_done, START + pair * 8 + 5 + b)
                    link(nc.vector.tensor_tensor(q_nat[:, b, :, :], ps[:, b, :].rearrange("p (l c) -> p l c", l=QT),
                                                 bq_row[:].unsqueeze(1).broadcast_to([P, QT, D]), ALU.add))
                    link.wait()
                    natural = q_nat[:, b, :, :].rearrange("p l (h d) -> p h l d", d=DK)
                    link(nc.vector.tensor_copy(q_split[:, b, :, 0, :, :], natural))
                    link.wait()
                    nc.vector.tensor_copy(q_split[:, b, :, 1, :, :], q_split[:, b, :, 0, :, :]).then_inc(q_split_ready, 1)
                    nc.vector.tensor_tensor(q_split[:, b, :, 2, :, :], natural, q_split[:, b, :, 0, :, :],
                                            ALU.subtract).then_inc(q_split_ready, 1)
                for b in range(2):
                    dve.wait_ge(proj_done, START + pair * 8 + 7 + b)
                    nc.vector.tensor_tensor(v_s[:, b * 4:b * 4 + 4, :], ps[:, 6 + b, :].rearrange("p (t c) -> p t c", t=RT),
                                            bv_row[:].unsqueeze(1).broadcast_to([P, RT, D]), ALU.add).then_inc(operands_ready, 1)
                return link.n

            def queries(pair, s):
                dve.wait_ge(score_done, START + pair * TILES + s * QUADS)
                for src, dst in ((q_hi, stat_hi), (q_lo, stat_lo)):
                    for b in range(2):
                        for half in range(2):
                            rows = src[:, bass.ds(b * L + s * ROWS, ROWS)].rearrange("p (q l) -> p q l", l=QT)
                            last = nc.vector.tensor_tensor(
                                dst[:, b, :, half, :].rearrange("p q (l h) -> p q l h", l=QT),
                                rows.unsqueeze(3).broadcast_to([P, QUADS, QT, DK]),
                                mask16h[:, half * 8:half * 8 + 8].unsqueeze(1).unsqueeze(1).broadcast_to([P, QUADS, QT, DK]), ALU.mult)
                last.then_inc(stat_ready, 1)

            def evacuate(pair, s, q):
                dve.wait_ge(tr_done, START + pair * TILES + s * QUADS + q + 1)
                nc.vector.tensor_copy(probs_t[:, q, :, :].rearrange("p r c -> p (r c)"), ps[:, 4 + q % 2, :]).then_inc(evac_dve, 1)

            def reciprocal(pair, s, q, first):
                dve.wait_ge(exp_done, START + pair * TILES + s * QUADS + q + 1)
                if not first:
                    dve.wait_ge(norm_done, START + pair * TILES + (s - 1) * QUADS + q + 1)
                nc.vector.reciprocal(inv_sum[:, q:q + 1], row_sum[:, q:q + 1]).then_inc(inv_done, 1)

            STEP_LINKS = 2

            def reduce_products(pair, s):
                link = Links(step_link, (pair * STEPS + s) * STEP_LINKS)
                dve.wait_ge(av_v_done, START + pair * STEPS + s + 1)
                link(nc.vector.tensor_tensor(v_masked[:], ps[:, 6, 0:256].rearrange("p (c h) -> p c h", h=4),
                                             m4.unsqueeze(1).broadcast_to([P, 2 * ROWS, 4]), ALU.mult))
                link.wait()
                for b in range(2):
                    last = nc.vector.tensor_reduce(attn_t[:, bass.ds(pair * TOK + b * L + s * ROWS, ROWS)],
                                                   v_masked[:, b * ROWS:(b + 1) * ROWS, :], op=ALU.add, axis=AX_X)
                last.then_inc(v_red, 1)
                dve.wait_ge(av_r_done, START + pair * STEPS + s + 1)
                link(nc.vector.tensor_tensor(r_masked[:], ps[:, 7, 0:256].rearrange("p (g l h) -> p g l h", l=QT, h=DK),
                                             m4.unsqueeze(1).unsqueeze(3).broadcast_to([P, 8, QT, DK]), ALU.mult))
                link.wait()
                nc.vector.tensor_reduce(rel_o[:].rearrange("p a (g h) -> p (a g) h", h=DK), r_masked[:].rearrange("p g l h -> p g h l"),
                                        op=ALU.add, axis=AX_X).then_inc(r_red, 1)

            def step(pair, s, first=False, last=False, more=True):
                for q in range(QUADS):
                    if not first and q in DVE_EVAC:
                        evacuate(pair, s - 1, q)
                    if not last:
                        dve.wait_ge(score_done, START + pair * TILES + s * QUADS + q + 1)
                        nc.vector.tensor_reduce(neg_max[:, q:q + 1], ps[:, q % S_BANKS, :], op=ALU.max, axis=AX_X,
                                                negate=True).then_inc(max_done, 1)
                        if q >= LAG:
                            reciprocal(pair, s, q - LAG, first)
                if not last:
                    for q in range(QUADS - LAG, QUADS):
                        reciprocal(pair, s, q, first)
                if more:
                    queries(pair, s + 1)
                if not first:
                    reduce_products(pair, s - 1)

            with dve.Fori(0, PAIRS) as pair:
                dve.wait_ge(tr_done, START + pair * TILES)
                assert prepare(pair) == PREP_LINKS
                dve.wait_ge(operands_ready, START + pair * 6 + 6)
                queries(pair, 0)
                step(pair, 0, first=True)
                with dve.Fori(1, STEPS - 1) as s:
                    step(pair, s)
                step(pair, STEPS - 1, more=False)
                step(pair, STEPS, last=True, more=False)

            FFN_LINKS = 13

            def prepare_attention(b, link):
                dve.wait_ge(rel_nat_tr, START + b + 1)
                nc.vector.tensor_tensor(o_sum_t, ps[:, 0, :], attn_t[:, bass.ds(b * L, L)], ALU.add).then_inc(o_ready, 1)

            def prepare_residual(b, slot, link):
                dve.wait_ge(wo_done, START + b + 1)
                rows = acc[:, slot, :, :]
                link(nc.vector.tensor_tensor(xn[:, 0:TPB, :], ps[:, 1, :].rearrange("p (t d) -> p t d", t=TPB),
                                             x_all[:, bass.ds(b * TPB, TPB), :], ALU.add))
                link.wait()
                link(nc.vector.tensor_tensor(rows, xn[:, 0:TPB, :], bo_row[:].unsqueeze(1).broadcast_to([P, TPB, D]), ALU.add))
                link.wait()
                for t in range(TPB):
                    last = nc.vector.bn_stats(stats[:, t, :], acc[:, slot, t, :])
                link(last)
                link.settle()
                for t in range(TPB):
                    last = nc.vector.bn_aggr(mv[:, t, :], stats[:, t, :])
                link(last)
                link.wait()
                nc.vector.tensor_scalar(var_eps[:, 0:TPB], mv[:, 0:TPB, 1], LN_EPS, None, ALU.add).then_inc(x1_var, 1)

            def prepare_norm(b, slot, link):
                dve.wait_ge(x1_rstd, START + b + 1)
                for t in range(TPB):
                    last = nc.vector.tensor_scalar(xn[:, t, :], acc[:, slot, t, :], mv[:, t, 0:1], rstd[:, t:t + 1],
                                                   ALU.subtract, ALU.mult)
                last.then_inc(hn_ready, 1)

            def prepare_gates(b, link):
                dve.wait_ge(gate_done, START + b + 1)
                link(nc.vector.tensor_tensor(gates[:], ps[:, 2, 0:TPB * NE].rearrange("p (t e) -> p t e", t=TPB),
                                             rb_row[:].unsqueeze(1).broadcast_to([P, TPB, NE]), ALU.add))
                link.settle()
                for t in range(TPB):
                    last = nc.vector.max(top8[:, t, :], gates[:, t, :])
                link(last)
                link.settle()
                for t in range(TPB):
                    last = nc.vector.max_index(top_i[:, t, :], top8[:, t, :], gates[:, t, :])
                link(last)
                link.wait()
                link(nc.vector.tensor_copy(top_f[:], top_i[:, :, 0:2]))
                nc.vector.tensor_tensor(gap[:], top8[:, :, 1], top8[:, :, 0], ALU.subtract).then_inc(gap_ready, 1)

            def prepare_comb(b, slot, link):
                dve.wait_ge(e_gap_ready, START + b + 1)
                link(nc.vector.tensor_scalar(prob2[:, :, 1], e_gap[:], 1.0, None, ALU.add))
                link.wait()
                link(nc.vector.reciprocal(prob2[:, :, 0], prob2[:, :, 1]))
                link.wait()
                link(nc.vector.tensor_tensor(prob2[:, :, 1], prob2[:, :, 0], e_gap[:], ALU.mult))
                link.wait()
                for t in range(TPB):
                    for j in range(2):
                        last = nc.vector.tensor_scalar(pick[:, t, j, :], iota8, top_f[:, t, j:j + 1], prob2[:, t, j:j + 1],
                                                       ALU.is_equal, ALU.mult)
                link(last)
                link.wait()
                nc.vector.tensor_tensor(comb[:, slot, :, NS:], pick[:, :, 0, :], pick[:, :, 1, :], ALU.add).then_inc(comb_ready, 1)

            def prepare_bias(b, slot, link):
                dve.wait_ge(bias_done, START + b + 1)
                link(nc.vector.tensor_tensor(acc[:, slot, :, :], ps[:, 3, :].rearrange("p (t d) -> p t d", t=TPB),
                                             acc[:, slot, :, :], ALU.add))
                link.wait()

            def expert(b, slot, e):
                dve.wait_ge(down_done, START + b * EXPERTS + e + 1)
                for t in range(TPB):
                    last = nc.vector.scalar_tensor_tensor(acc[:, slot, t, :], ps[:, 6 + e % 2, t * D:(t + 1) * D],
                                                          comb[:, slot, t, e:e + 1], acc[:, slot, t, :], ALU.mult, ALU.add)
                last.then_inc(final_ready if e == EXPERTS - 1 else y_used, 1)
                if e < EXPERTS - 1:
                    dve.wait_ge(y_used, START + b * (EXPERTS - 1) + e + 1)
                else:
                    dve.wait_ge(final_ready, START + b + 1)

            def batch(b, slot, ahead):
                link = Links(ffn_link, (b + 1) * FFN_LINKS)
                for e in range(EXPERTS):
                    expert(b, slot, e)
                    if ahead:
                        if e == 0:
                            prepare_attention(b + 1, link)
                        if e == 2:
                            dve.wait_ge(stored, START + (b + 1 - 1) * 16)
                            prepare_residual(b + 1, 1 - slot, link)
                        if e == 3:
                            prepare_norm(b + 1, 1 - slot, link)
                        if e == 6:
                            prepare_gates(b + 1, link)
                        if e == 7:
                            prepare_comb(b + 1, 1 - slot, link)
                        if e == 9:
                            prepare_bias(b + 1, 1 - slot, link)
                assert not ahead or link.n == FFN_LINKS, link.n

            link = Links(ffn_link, 0)
            prepare_attention(0, link)
            prepare_residual(0, 0, link)
            prepare_norm(0, 0, link)
            prepare_gates(0, link)
            prepare_comb(0, 0, link)
            prepare_bias(0, 0, link)
            assert link.n == FFN_LINKS, link.n
            with dve.Fori(0, B // 2 - 1) as i:
                batch(2 * i, 0, True)
                batch(2 * i + 1, 1, True)
            batch(B - 2, 0, True)
            batch(B - 1, 1, False)

        @block.tensor
        def _(pe):
            pe.wait_ge(loaded, 16 * LOADS)
            pe.wait_ge(setup_dve, SETUP_DVE)

            def prepare(pair):
                for half in range(2):
                    pe.wait_ge(xn_ready, START + pair * 8 + half * 4 + 4)
                    for t in range(4):
                        last = nc.tensor.transpose(ps[:, half, t * P:(t + 1) * P], xn[:, half * 4 + t, :], ident)
                    last.then_inc(xn_tr, 1)
                pe.wait_ge(xn_t_ready, START + pair * 2 + 2)
                for n, w in enumerate((wq_s, wq_s, wk_s, wk_s)):
                    nc.tensor.matmul(ps[:, 2 + n, :], w[:], xn_t[:, (n % 2) * L:(n % 2 + 1) * L], start=True, stop=True).then_inc(proj_done, 1)
                for b in range(2):
                    for l in range(QT):
                        rows = xn_t[:, b * L:(b + 1) * L].rearrange("p (q l) -> p l q", l=QT)[:, l, :]
                        last = nc.tensor.matmul(ps[:, b, l * D:(l + 1) * D], rows, wq_s[:], start=True, stop=True)
                    last.then_inc(proj_done, 1)
                for b in range(2):
                    for t in range(RT):
                        last = nc.tensor.matmul(ps[:, 6 + b, t * D:(t + 1) * D], xn_t[:, b * L + t * P:b * L + (t + 1) * P], wv_s[:],
                                                start=True, stop=True)
                    last.then_inc(proj_done, 1)
                pe.wait_ge(operands_ready, START + pair * 6 + 4)
                for b in range(2):
                    pe.wait_ge(q_split_ready, START + pair * 4 + b * 2 + 2)
                    for half in range(2):
                        for h in range(8):
                            pieces = q_split[:, b, half * 8 + h, :, :, :].rearrange("p a l d -> p (a l d)")
                            last = nc.tensor.transpose(bank_h(2 + b * 2 + half, 8 * P)[0:REL_K, h * P:(h + 1) * P], pieces, identh[:])
                        last.then_inc(q_rel_tr, 1)
                pe.wait_ge(q_rel_ready, START + pair * 4 + 4)
                pe.wait_ge(operands_ready, START + pair * 6 + 6)

            def scores(pair, s, q, first):
                if q == 0:
                    pe.wait_ge(stat_ready, START + pair * STEPS + s + 1)
                    pe.wait_ge(stat_rel_ready, START + pair * STEPS + s + 1)
                    pe.wait_ge(rk_landed, START + (pair * STEPS + s + 1) * 16)
                if not (first and q < S_BANKS):
                    pe.wait_ge(exp_done, START + pair * TILES + s * QUADS + q - S_BANKS + 1)
                bank = ps[:, q % S_BANKS, :]
                window = (ROWS - QT) - QT * q
                nc.tensor.matmul(bank, stat_rel[:, q, :, :, :].rearrange("k g l h -> k (g l h)"), rk_step[:, window:window + L],
                                 start=True, stop=False, skip_group_check=True)
                for stat, keys in ((stat_hi, k_hi), (stat_hi, k_lo), (stat_lo, k_hi)):
                    for b in range(2):
                        last = nc.tensor.matmul(ps[b * 64:b * 64 + 64, q % S_BANKS, :], stat[:, b, q, :, :].rearrange("p a c -> p (a c)"),
                                                keys[:, b * L:(b + 1) * L], start=False, stop=stat is stat_lo, skip_group_check=True)
                last.then_inc(score_done, 1)

            def transposes(pair, s, q):
                pe.wait_ge(norm_done, START + pair * TILES + s * QUADS + q + 1)
                if q >= 2:
                    if q - 2 in ACT_EVAC:
                        pe.wait_ge(evac_act, START + (pair * STEPS + s) * len(ACT_EVAC) + ACT_EVAC.index(q - 2) + 1)
                    else:
                        pe.wait_ge(evac_dve, START + (pair * STEPS + s) * len(DVE_EVAC) + DVE_EVAC.index(q - 2) + 1)
                for rt in range(RT):
                    last = nc.tensor.transpose(ps[:, 4 + q % 2, rt * P:(rt + 1) * P], probs[:, q, rt * P:(rt + 1) * P], ident)
                last.then_inc(tr_done, 1)

            def products(pair, s, first):
                pe.wait_ge(evac_act, START + (pair * STEPS + s + 1) * len(ACT_EVAC))
                pe.wait_ge(evac_dve, START + (pair * STEPS + s + 1) * len(DVE_EVAC))
                pe.wait_ge(v_red, START + pair * STEPS + s)
                pe.wait_ge(rel_t_ready, START + pair * STEPS + s)
                for b in range(2):
                    for rt in range(RT):
                        for g in range(4):
                            at = b * 64 + (g // 2) * 32
                            cols = probs_t[:, :, rt, at:at + 32].rearrange("p q (l h) -> p q l h", l=QT)[:, :, :, (g % 2) * 4:(g % 2) * 4 + 4]
                            last = nc.tensor.matmul(ps[32 * g:32 * g + 32, 6, b * P:(b + 1) * P], v_s[:, b * 4 + rt, 32 * g:32 * g + 32], cols,
                                                    start=rt == 0, stop=rt == RT - 1, skip_group_check=True)
                last.then_inc(av_v_done, 1)
                pe.wait_ge(rv_landed, START + (pair * STEPS + s + 1) * 16)
                pe.wait_ge(r_red, START + pair * STEPS + s)
                for half in range(2):
                    for rt in range(RT):
                        for g in range(4):
                            q = half * 4 + g
                            last = nc.tensor.matmul(ps[32 * g:32 * g + 32, 7, half * P:(half + 1) * P], rv_step[:, RT - 1 - rt, q * 32:q * 32 + 32],
                                                    probs_t[:, q, rt, :], start=rt == 0, stop=rt == RT - 1, skip_group_check=True)
                last.then_inc(av_r_done, 1)

            def rel_transposes(pair, s):
                pe.wait_ge(r_red, START + pair * STEPS + s + 1)
                pe.wait_ge(v_red, START + pair * STEPS + s + 1)
                for half in range(2):
                    last = nc.tensor.transpose(ps[0:32, 6, 256 + half * P:256 + (half + 1) * P], rel_o[:, half, :], ident)
                last.then_inc(rel_tr, 1)

            def step(pair, s, first=False, rel=True, last=False):
                for q in range(QUADS):
                    if not first:
                        transposes(pair, s - 1, q)
                    if rel and q == 4:
                        rel_transposes(pair, s - 2)
                    if not last:
                        scores(pair, s, q, first)
                if not first:
                    products(pair, s - 1, False)

            with pe.Fori(0, PAIRS) as pair:
                prepare(pair)
                step(pair, 0, first=True, rel=False)
                step(pair, 1, rel=False)
                with pe.Fori(2, STEPS) as s:
                    step(pair, s)
                step(pair, STEPS, last=True)
                rel_transposes(pair, STEPS - 1)
                pe.wait_ge(rel_t_ready, START + (pair + 1) * STEPS)

            def prepare_attention(b):
                pe.wait_ge(rel_landed, START + (b + 1) * 16 * TPB)
                for t in range(TPB):
                    last = nc.tensor.transpose(ps[:, 0, t * P:(t + 1) * P], rel_nat[:, t, :, :].rearrange("p h d -> p (h d)"), ident)
                last.then_inc(rel_nat_tr, 1)

            def prepare_output(b):
                pe.wait_ge(o_ready, START + b + 1)
                for t in range(TPB):
                    last = nc.tensor.matmul(ps[:, 1, t * D:(t + 1) * D], o_sum_t[:, t * P:(t + 1) * P], wo_s[:], start=True, stop=True)
                last.then_inc(wo_done, 1)

            def prepare_h(b):
                pe.wait_ge(hn_ready, START + b + 1)
                for t in range(TPB):
                    last = nc.tensor.transpose(ps[:, 0, t * P:(t + 1) * P], xn[:, t, :], ident)
                last.then_inc(hn_tr, 1)

            def prepare_gates(b, slot):
                pe.wait_ge(h_ready, START + b + 1)
                for t in range(TPB):
                    last = nc.tensor.matmul(ps[:, 2, t * NE:(t + 1) * NE], h_t[:, slot, t * P:(t + 1) * P], rw_s[:], start=True, stop=True)
                last.then_inc(gate_done, 1)

            def prepare_comb(b, slot):
                pe.wait_ge(comb_ready, START + b + 1)
                for t in range(TPB):
                    last = nc.tensor.transpose(ps[0:EXPERTS, 1, t * P:(t + 1) * P], comb[:, slot, t, :], ident)
                last.then_inc(comb_tr, 1)

            def prepare_bias(b):
                pe.wait_ge(comb_t_ready, START + b + 1)
                for t in range(TPB):
                    last = nc.tensor.matmul(ps[:, 3, t * D:(t + 1) * D], comb_t[:, t * P:(t + 1) * P], b2_s[:], start=True, stop=True)
                last.then_inc(bias_done, 1)

            def up(b, slot, e):
                for k in range(2):
                    pe.wait_ge(gelu_done, START + b * 20 + (e * 2 + k - 1 if e else 0))
                    nc.tensor.matmul(ps[:, 4 + k, :], w1_s[:, e, k * P:(k + 1) * P], h_t[:, slot, :], start=True, stop=True).then_inc(up_done, 1)

            def down(b, e):
                pe.wait_ge(gelu_done, START + b * 20 + e * 2 + 2)
                if e >= 2:
                    pe.wait_ge(y_used, START + b * (EXPERTS - 1) + e - 1)
                else:
                    pe.wait_ge(final_ready, START + b)
                for t in range(TPB):
                    for k in range(2):
                        last = nc.tensor.matmul(ps[:, 6 + e % 2, t * D:(t + 1) * D], hid[:, e % 2, k, t * P:(t + 1) * P], w2_s[:, e, k, :],
                                                start=k == 0, stop=k == 1)
                last.then_inc(down_done, 1)

            def batch(b, slot, ahead):
                up(b, slot, 0)
                for e in range(EXPERTS):
                    if e + 1 < EXPERTS:
                        up(b, slot, e + 1)
                    down(b, e)
                    if ahead:
                        if e == 0:
                            prepare_attention(b + 1)
                        if e == 1:
                            prepare_output(b + 1)
                        if e == 4:
                            prepare_h(b + 1)
                        if e == 5:
                            prepare_gates(b + 1, 1 - slot)
                        if e == 8:
                            prepare_comb(b + 1, 1 - slot)
                        if e == 9:
                            prepare_bias(b + 1)

            prepare_attention(0)
            prepare_output(0)
            prepare_h(0)
            prepare_gates(0, 0)
            prepare_comb(0, 0)
            prepare_bias(0)
            with pe.Fori(0, B // 2 - 1) as i:
                batch(2 * i, 0, True)
                batch(2 * i + 1, 1, True)
            batch(B - 2, 0, True)
            batch(B - 1, 1, False)


def relative_windows(table_k, table_v):
    n = 2 * MAX_LEN - 1

    def at(apart):
        index = apart + MAX_LEN - 1
        return np.clip(np.where(index < 0, index + n, index), 0, n - 1)

    rows, cols = np.arange(QT)[:, None], np.arange(RK_COLS)[None, :]
    keys = table_k[at(cols - (L - QT) - rows)]
    rk = np.ascontiguousarray(keys.transpose(0, 2, 1).reshape(QT * DK, RK_COLS))
    part, cols = np.arange(P)[:, None], np.arange(RV_COLS)[None, :]
    rv = np.ascontiguousarray(table_v[at(part - cols + (L - P))].reshape(P, RV_COLS * DK))
    return rk, rv


def constants():
    row = np.arange(P)[:, None]
    c = np.zeros((P, CONSTS), np.float32)
    c[:, M4:M4 + 4] = (row // DK) % 4 == np.arange(4)[None, :]
    c[:, M16:M16 + H] = row // DK == np.arange(H)[None, :]
    c[:, IOTA:IOTA + NE] = np.arange(NE)[None, :]
    c[:, IDENT:] = np.eye(P)
    return c


def kernel(**inputs):
    import concourse.bacc as bacc
    from concourse.bass_utils import run_bass_kernel_spmd

    given = {name: np.asarray(a) for name, a in inputs.items()}
    rk, rv = relative_windows(given["L0_attn_relative_k"], given["L0_attn_relative_v"])
    arrays = {"x": given["L0_attn_x"].reshape(B * L, D)}
    for name in ("Wq", "Wk", "Wv", "Wo"):
        arrays[name.lower() + "_t"] = given["L0_attn_" + name].T
    for name in ("bq", "bk", "bv", "bo"):
        arrays[name] = given["L0_attn_" + name]
    arrays |= {"rk_win": rk, "rv_win": rv}
    for name, short in (("router_w", "rw"), ("router_b", "rb"), ("w1", "w1"), ("w2", "w2"), ("b2", "b2"),
                        ("sw1", "sw1"), ("sw2", "sw2"), ("sb2", "sb2")):
        arrays[short] = given["L0_ffn_" + name]
    b1 = np.concatenate([given["L0_ffn_sb1"], given["L0_ffn_b1"]])
    arrays["b1_cols"] = b1.reshape(EXPERTS, 2, P).transpose(2, 0, 1)
    arrays["consts"] = constants()

    nc = bacc.Bacc("TRN2", target_bir_lowering=False, num_devices=1)
    args, in_map = [], {}
    for name, a in arrays.items():
        a = np.ascontiguousarray(a)
        in_map["in_" + name] = a
        args.append(nc.dram_tensor("in_" + name, a.shape, mybir.dt.from_np(a.dtype), kind="ExternalInput").ap())
    args.append(nc.dram_tensor("rel_scratch", (B * H, L * DK), F32, kind="Internal").ap())
    args.append(nc.dram_tensor("out", (B * L, D), F32, kind="ExternalOutput").ap())
    attention_ffn(nc, *args)
    r = run_bass_kernel_spmd(nc, [in_map], core_ids=[0])
    return r.results[0]["out"].reshape(B, L, D)
```

```python
import math
from contextlib import ExitStack

import numpy as np

import concourse.bass as bass
from concourse import mybir

F32 = mybir.dt.float32
F16 = mybir.dt.float16
U32 = mybir.dt.uint32
U8 = mybir.dt.uint8
ALU = mybir.AluOpType
ACT = mybir.ActivationFunctionType
AX_X = mybir.AxisListType.X

P = 128
B, L, D = 16, 512, 128
H, DK = 16, 8
MAX_LEN = 128
NE, NS, HID = 8, 2, 256
EXPERTS = NS + NE
LN_EPS = 1e-5
SCALE = float(np.float32(1.0) / np.sqrt(DK).astype(np.float32))

PAIRS = B // 2
TOK = 2 * L
QT = 4
QUADS = 8
ROWS = QT * QUADS
STEPS = L // ROWS
RT = L // P
TILES = STEPS * QUADS
REL_K = 3 * QT * DK
WIN = L + ROWS - QT
RK_COLS = 2 * L - QT
RV_COLS = (L - ROWS) + L
NT = B * L // P
TPB = L // P
S_BANKS = 4
START = 1
LAG = 2
ACT_EVAC = (0, 1, 2, 4, 5, 6)
DVE_EVAC = (3, 7)
M4, M16, IOTA, M8 = 0, 4, 20, 28
IDENT = 36
CONSTS = IDENT + P


def attention_ffn(nc, x, wq_t, wk_t, wv_t, wo_t, bq, bk, bv, bo, rk_win, rv_win, rw, rb, w1, w2, b2,
                  sw1, sw2, sb2, b1_cols, consts, rel_scratch, out):
    with ExitStack() as ctx:
        def sb(name, shape, dt=F32):
            return ctx.enter_context(nc.sbuf_tensor(name, shape, dt))

        def sem(name):
            return ctx.enter_context(nc.semaphore(name))

        ps = ctx.enter_context(nc.psum_tensor("ps", [P, 8, 512], F32))

        x_pair = sb("x_pair", [P, 8, D])
        x_batch = x_pair[:, 0:TPB, :]
        attn_t = sb("attn_t", [P, B * L])
        const = sb("const", [P, CONSTS])
        m4, iota8, ident = const[:, M4:M4 + 4], const[:, IOTA:IOTA + NE], const[:, IDENT:IDENT + P]
        mask16h = sb("mask16h", [P, H], F16)
        mask8h = sb("mask8h", [P, DK], F16)
        mask4h = sb("mask4h", [P, QT, DK], F16)
        identh = sb("identh", [P, P], F16)
        wq_s, wk_s, wv_s, wo_s = (sb(n, [P, D]) for n in ("wq_s", "wk_s", "wv_s", "wo_s"))
        bq_col, bk_col, bks_col = (sb(n, [P, 1]) for n in ("bq_col", "bk_col", "bks_col"))
        bq_row, bv_row, bo_row = (sb(n, [P, D]) for n in ("bq_row", "bv_row", "bo_row"))
        rk3 = sb("rk3", [REL_K, RK_COLS])
        rk_split = sb("rk_split", [REL_K, RK_COLS], F16)
        rw_s = sb("rw_s", [P, NE])
        rb_row = sb("rb_row", [P, NE])
        w1_s = sb("w1_s", [P, EXPERTS, HID])
        w2_s = sb("w2_s", [P, EXPERTS, 2, D])
        b1_s = sb("b1_s", [P, EXPERTS, 2])
        b2_s = sb("b2_s", [EXPERTS, D])
        half_pow = sb("half_pow", [P, 8])
        e_const = sb("e_const", [P, TPB])

        settled = sb("settled", [P, 1])
        stats = sb("stats", [P, 8, 6])
        mv = sb("mv", [P, 8, 2])
        var_eps = sb("var_eps", [P, 8])
        rstd = sb("rstd", [P, 8])
        xn = sb("xn", [P, 8, D])
        xn_t = sb("xn_t", [P, TOK])
        q_hi, q_lo, k_hi, k_lo = (sb(n, [P, TOK], F16) for n in ("q_hi", "q_lo", "k_hi", "k_lo"))
        q_twice, k_both = (sb(n, [P, 2, TOK], F16) for n in ("q_twice", "k_both"))
        v_s = sb("v_s", [P, 8, D])
        q_nat = sb("q_nat", [P, 2, QT, D])
        q_split = sb("q_split", [P, 2, H, 3, QT, DK], F16)
        q_rel = sb("q_rel", [REL_K, P, 4, DK], F16)

        stat_hi = sb("stat_hi", [P, 2, 2, QUADS, ROWS], F16)
        stat_lo = sb("stat_lo", [P, 2, QUADS, 2, ROWS], F16)
        stat_rel = sb("stat_rel", [REL_K, QUADS, 4, QT, DK], F16)
        rk_step = sb("rk_step", [REL_K, WIN], F16)
        rv_step = sb("rv_step", [P, RT, ROWS * DK])
        neg_max = sb("neg_max", [P, QUADS])
        row_sum = sb("row_sum", [P, QUADS])
        inv_sum = sb("inv_sum", [P, QUADS])
        probs = sb("probs", [P, QUADS, L])
        probs_t = sb("probs_t", [P, QUADS, RT, P])
        v_masked = sb("v_masked", [P, 2 * ROWS, 4])
        r_masked = sb("r_masked", [P, 8, QT, DK])
        rel_o = sb("rel_o", [P, 2, 32])
        rel_t = sb("rel_t", [32, STEPS, 2, P])

        rel_nat = v_s[:, 0:TPB, :].rearrange("p t (h d) -> p t h d", h=H)
        o_sum_t = xn_t[:, 0:L]
        h_t = q_nat[:].rearrange("p b l c -> p b (l c)")
        gates = sb("gates", [P, TPB, NE])
        top8 = sb("top8", [P, TPB, 8])
        top_i = sb("top_i", [P, TPB, 8], U32)
        top_f = sb("top_f", [P, TPB, 2])
        gap = sb("gap", [P, TPB])
        e_gap = sb("e_gap", [P, TPB])
        prob2 = sb("prob2", [P, TPB, 2])
        pick = sb("pick", [P, TPB, 2, NE])
        comb = sb("comb", [P, 2, TPB, EXPERTS])
        comb_t = sb("comb_t", [EXPERTS, L])
        acc = sb("acc", [P, 2, TPB, D])
        hid = probs[:, 0:4, :].rearrange("p (e k) c -> p e k c", e=2)

        loaded = sem("loaded")
        setup_dve = sem("setup_dve")
        setup_pool = sem("setup_pool")
        x_landed, q_twice_landed, k_both_landed = sem("x_landed"), sem("q_twice_landed"), sem("k_both_landed")
        x_batch_landed = sem("x_batch_landed")
        var_ready, rstd_ready, xn_ready, xn_tr = sem("var_ready"), sem("rstd_ready"), sem("xn_ready"), sem("xn_tr")
        xn_t_ready, proj_done, hi_ready = sem("xn_t_ready"), sem("proj_done"), sem("hi_ready")
        dve_link, ln_link = sem("dve_link"), sem("ln_link")
        operands_ready, q_split_ready, q_rel_tr = sem("operands_ready"), sem("q_split_ready"), sem("q_rel_tr")
        q_rel_ready = sem("q_rel_ready")
        stat_ready, stat_rel_ready = sem("stat_ready"), sem("stat_rel_ready")
        rk_landed, rv_landed = sem("rk_landed"), sem("rv_landed")
        score_done, max_done, exp_done, inv_done = sem("score_done"), sem("max_done"), sem("exp_done"), sem("inv_done")
        norm_done, tr_done, evac_act, evac_dve = sem("norm_done"), sem("tr_done"), sem("evac_act"), sem("evac_dve")
        av_v_done, av_r_done, v_red, r_red = sem("av_v_done"), sem("av_r_done"), sem("v_red"), sem("r_red")
        step_link = sem("step_link")
        rel_tr, rel_t_ready, rel_stored = sem("rel_tr"), sem("rel_t_ready"), sem("rel_stored")
        rel_landed, rel_nat_tr, o_ready, wo_done = sem("rel_landed"), sem("rel_nat_tr"), sem("o_ready"), sem("wo_done")
        ffn_link, x1_var, x1_rstd = sem("ffn_link"), sem("x1_var"), sem("x1_rstd")
        hn_ready, hn_tr, h_ready = sem("hn_ready"), sem("hn_tr"), sem("h_ready")
        gate_done, gap_ready, e_gap_ready, comb_ready = sem("gate_done"), sem("gap_ready"), sem("e_gap_ready"), sem("comb_ready")
        comb_tr, comb_t_ready, bias_done, acc_ready = sem("comb_tr"), sem("comb_t_ready"), sem("bias_done"), sem("acc_ready")
        up_done, gelu_done, down_done, y_used = sem("up_done"), sem("gelu_done"), sem("down_done"), sem("y_used")
        final_ready, stored = sem("final_ready"), sem("stored")

        LOADS = 24
        SETUP_DVE = 8
        SETUP_POOL = 3

        counted = (ln_link, x_landed, q_twice_landed, k_both_landed, x_batch_landed, av_r_done, av_v_done, bias_done, comb_ready, comb_t_ready, comb_tr, down_done, dve_link,
                   e_gap_ready, evac_act, evac_dve, exp_done, ffn_link, final_ready, gap_ready, gate_done,
                   gelu_done, h_ready, hi_ready, hn_ready, hn_tr, inv_done, max_done, norm_done,
                   o_ready, operands_ready, proj_done, q_rel_ready, q_rel_tr, q_split_ready, r_red, rel_landed,
                   rel_nat_tr, rel_stored, rel_t_ready, rel_tr, rk_landed, rstd_ready, rv_landed, score_done,
                   stat_ready, stat_rel_ready, step_link, stored, tr_done, up_done, v_red, var_ready,
                   wo_done, x1_rstd, x1_var, xn_ready, xn_t_ready, xn_tr, y_used)

        block = ctx.enter_context(nc.Block())

        def bank_h(bank, n):
            return ps[:, bank, :].bitcast(F16)[:, 0:n]

        @block.sync
        def _(sp):
            for semaphore in counted:
                sp.sem_inc(semaphore, START)

            def load(dst, src):
                sp.dma_start(dst, src).then_inc(loaded, 16)

            x_rows = x.rearrange("(n t p) d -> n p t d", t=8, p=P)
            sp.dma_start(x_pair[:], x_rows[0, :, :, :]).then_inc(x_landed, 16)
            load(const[:], consts)
            for dst, src in ((wq_s, wq_t), (wk_s, wk_t), (wv_s, wv_t), (wo_s, wo_t)):
                load(dst[:], src)
            for dst, src in ((bq_col, bq), (bk_col, bk)):
                load(dst[:], src.rearrange("(p a) -> p a", a=1))
            for dst, src in ((bq_row, bq), (bv_row, bv), (bo_row, bo), (rb_row, rb)):
                load(dst[:], src.partition_broadcast(P))
            for piece in range(3):
                load(rk3[piece * 32:piece * 32 + 32, :], rk_win)
            load(rw_s[:], rw)
            load(w1_s[:, 0:NS, :], sw1.rearrange("e d h -> d e h"))
            load(w1_s[:, NS:, :], w1.rearrange("e d h -> d e h"))
            for k in range(2):
                load(w2_s[:, 0:NS, k, :], sw2[:, k * P:(k + 1) * P, :].rearrange("e h d -> h e d"))
                load(w2_s[:, NS:, k, :], w2[:, k * P:(k + 1) * P, :].rearrange("e h d -> h e d"))
            load(b1_s[:], b1_cols)
            load(b2_s[0:NS, :], sb2)
            load(b2_s[NS:, :], b2)

            def value_window(s, multiplied):
                at = sp.snap(sp.to_reg(ROWS * DK * 4 * s))
                blocks = rv_win.bitcast(U8)[:, bass.ds(at, RT * P * DK * 4)].rearrange("p (t c) -> p t c", t=RT)
                sp.wait_ge(av_r_done, START + multiplied)
                sp.dma_start(rv_step[:].bitcast(U8), blocks[:, :, 0:ROWS * DK * 4]).then_inc(rv_landed, 16)

            def double(pair):
                sp.wait_ge(hi_ready, START + pair * 4 + 2)
                for half in range(2):
                    for copy in range(2):
                        sp.dma_start(q_twice[64 * copy:64 * copy + 64, half, :], q_hi[64 * half:64 * half + 64, :]).then_inc(q_twice_landed, 16)
                sp.wait_ge(hi_ready, START + pair * 4 + 4)
                sp.wait_ge(operands_ready, START + pair * 6 + 4)
                for half in range(2):
                    for piece, keys in enumerate((k_hi, k_lo)):
                        sp.dma_start(k_both[64 * piece:64 * piece + 64, half, :], keys[64 * half:64 * half + 64, :]).then_inc(k_both_landed, 16)

            def pair_windows(pair, ahead):
                with sp.Fori(0, STEPS) as s:
                    value_window(s, pair * STEPS + s)
                if ahead:
                    double(pair + 1)
                row = sp.snap(sp.to_reg(pair * 32))
                sp.wait_ge(rel_t_ready, START + (pair + 1) * STEPS)
                sp.dma_start(rel_scratch[bass.ds(row, 32), :], rel_t[:].rearrange("p s a c -> p (s a c)")).then_inc(rel_stored, 16)

            def next_rows(pair):
                following = sp.snap(sp.to_reg(pair + 1))
                sp.wait_ge(xn_ready, START + pair * 8 + 8)
                sp.dma_start(x_pair[:], x_rows[bass.ds(following, 1), :, :, :].rearrange("n p t d -> (n p) t d")).then_inc(x_landed, 16)

            double(0)
            with sp.Fori(0, PAIRS - 1) as pair:
                next_rows(pair)
                pair_windows(pair, True)
            pair_windows(PAIRS - 1, False)
            sp.wait_ge(rel_stored, START + PAIRS * 16)

            rel_rows = rel_scratch.rearrange("(b h) (t p d) -> b t p h d", h=H, p=P, d=DK)

            batch_rows = x.rearrange("(n t p) d -> n p t d", t=TPB, p=P)

            def load_rel(b):
                sp.dma_start(x_batch, batch_rows[bass.ds(b, 1), :, :, :].rearrange("n p t d -> (n p) t d")).then_inc(x_batch_landed, 16)
                for t in range(TPB):
                    sp.dma_start(rel_nat[:, t, :, :], rel_rows[bass.ds(b, 1), t, :, :, :].rearrange("b p h d -> (b p) h d")).then_inc(rel_landed, 16)

            load_rel(0)
            out_rows = out.rearrange("(b t p) d -> b p t d", t=TPB, p=P)

            def store(b, slot):
                b = sp.snap(sp.to_reg(b))
                sp.wait_ge(final_ready, START + b + 1)
                sp.dma_start(out_rows[bass.ds(b, 1), :, :, :].rearrange("b p t d -> (b p) t d"), acc[:, slot, :, :]).then_inc(stored, 16)

            with sp.Fori(0, B // 2 - 1) as i:
                for slot in range(2):
                    following = sp.snap(sp.to_reg(2 * i + slot + 1))
                    sp.wait_ge(rel_nat_tr, START + following)
                    sp.wait_ge(x1_var, START + following)
                    load_rel(following)
                    store(2 * i + slot, slot)
            sp.wait_ge(rel_nat_tr, START + B - 1)
            sp.wait_ge(x1_var, START + B - 1)
            load_rel(B - 1)
            store(B - 2, 0)
            store(B - 1, 1)
            sp.wait_ge(stored, START + 16 * B)

        @block.gpsimd
        def _(pool):
            nc.gpsimd.memset(half_pow[:], -0.5).then_inc(setup_pool, 1)
            nc.gpsimd.memset(e_const[:], math.e).then_inc(setup_pool, 1)
            nc.gpsimd.memset(comb[:], 1.0 / NS).then_inc(setup_pool, 1)
            pool.wait_ge(setup_pool, SETUP_POOL)
            pool.wait_ge(setup_dve, SETUP_DVE)

            def relative_queries(s):
                quads = q_rel[:, bass.ds(s * QUADS, QUADS), :, :].rearrange("k q g h -> k (q g) h")
                nc.gpsimd.tensor_tensor(
                    stat_rel[:].rearrange("k q g l h -> k (q g) l h"),
                    quads.unsqueeze(2).broadcast_to([REL_K, QUADS * 4, QT, DK]),
                    mask4h[0:REL_K].unsqueeze(1).broadcast_to([REL_K, QUADS * 4, QT, DK]), ALU.mult).then_inc(stat_rel_ready, 1)

            def normalise(done, q):
                pool.wait_ge(inv_done, START + done + q + 1)
                nc.gpsimd.tensor_tensor(probs[:, q, :], probs[:, q, :], inv_sum[:, q:q + 1].broadcast_to([P, L]),
                                        ALU.mult).then_inc(norm_done, 1)

            def deviations(pair):
                pool.wait_ge(var_ready, START + pair + 1)
                nc.gpsimd.tensor_tensor(rstd[:], var_eps[:], half_pow[:], ALU.pow).then_inc(rstd_ready, 1)

            def pair_steps(pair, ahead):
                pool.wait_ge(q_rel_ready, START + (pair + 1) * 4)
                relative_queries(0)
                with pool.Fori(0, STEPS - 1) as s:
                    for q in range(QUADS):
                        if q == 6:
                            pool.wait_ge(score_done, START + pair * TILES + (s + 1) * QUADS)
                            relative_queries(s + 1)
                        normalise(pair * TILES + s * QUADS, q)
                for q in range(QUADS):
                    normalise(pair * TILES + (STEPS - 1) * QUADS, q)
                if ahead:
                    deviations(pair + 1)

            deviations(0)
            with pool.Fori(0, PAIRS - 1) as pair:
                pair_steps(pair, True)
            pair_steps(PAIRS - 1, False)

            def prepare(b):
                pool.wait_ge(x1_var, START + b + 1)
                nc.gpsimd.tensor_tensor(rstd[:, 0:TPB], var_eps[:, 0:TPB], half_pow[:, 0:TPB], ALU.pow).then_inc(x1_rstd, 1)
                pool.wait_ge(gap_ready, START + b + 1)
                nc.gpsimd.tensor_tensor(e_gap[:], e_const[:], gap[:], ALU.pow).then_inc(e_gap_ready, 1)

            with pool.Fori(0, B) as b:
                prepare(b)

        @block.scalar
        def _(act):
            act.wait_ge(loaded, 16 * LOADS)
            act.wait_ge(setup_dve, SETUP_DVE)

            def rows_t(pair):
                for half in range(2):
                    act.wait_ge(xn_tr, START + pair * 2 + half + 1)
                    nc.scalar.activation(xn_t[:, half * L:(half + 1) * L], ps[:, half, :], ACT.Copy).then_inc(xn_t_ready, 1)

            def high_halves(pair, n, hi, bias, bank):
                for b in range(2):
                    act.wait_ge(proj_done, START + pair * 8 + n + b + 1)
                    nc.scalar.activation(hi[:, b * L:(b + 1) * L], ps[:, bank + b, :], ACT.Identity,
                                         bias=bias[:, 0:1]).then_inc(hi_ready, 1)

            def relative_queries(pair, b):
                for half in range(2):
                    n = b * 2 + half
                    act.wait_ge(q_rel_tr, START + pair * 4 + n + 1)
                    nc.scalar.activation(q_rel[:, :, n, :], bank_h(n, 8 * P)[0:REL_K, :].rearrange("k (h q) -> k q h", h=DK),
                                         ACT.Copy).then_inc(q_rel_ready, 1)

            def key_window(pair, s):
                act.wait_ge(score_done, START + pair * TILES + s * QUADS)
                act.dma_start(rk_step[:], rk_split[:, bass.ds(L - ROWS - ROWS * s, WIN)]).then_inc(rk_landed, 16)

            def evacuate(pair, s, q):
                act.wait_ge(tr_done, START + pair * TILES + s * QUADS + q + 1)
                nc.scalar.activation(probs_t[:, q, :, :].rearrange("p r c -> p (r c)"), ps[:, 4 + q % 2, :], ACT.Copy).then_inc(evac_act, 1)

            def exponentials(pair, s, q, first):
                act.wait_ge(max_done, START + pair * TILES + s * QUADS + q + 1)
                if not first:
                    act.wait_ge(tr_done, START + pair * TILES + (s - 1) * QUADS + q + 1)
                nc.scalar.activation(probs[:, q, :], ps[:, q % S_BANKS, :], ACT.Exp, bias=neg_max[:, q:q + 1],
                                     accum_out=row_sum[:, q:q + 1]).then_inc(exp_done, 1)

            def rel_out(pair, s):
                act.wait_ge(rel_tr, START + pair * STEPS + s + 1)
                nc.scalar.activation(rel_t[:, bass.ds(s, 1), :, :].rearrange("p s a c -> p (s a c)"), ps[0:32, 6, 256:512],
                                     ACT.Copy).then_inc(rel_t_ready, 1)

            def step(pair, s, first=False, rel=True):
                for q in range(QUADS):
                    if not first and q in ACT_EVAC:
                        evacuate(pair, s - 1, q)
                    if rel and q == 5:
                        rel_out(pair, s - 2)
                    if q:
                        exponentials(pair, s, q - 1, first)
                exponentials(pair, s, QUADS - 1, first)

            def last_step(pair, ahead):
                for q in range(QUADS):
                    if q in ACT_EVAC:
                        evacuate(pair, STEPS - 1, q)
                    if q == 5:
                        rel_out(pair, STEPS - 2)
                    if ahead:
                        if q == 1:
                            rows_t(pair + 1)
                        if q == 3:
                            high_halves(pair + 1, 0, q_hi, bq_col, 2)
                        if q == 5:
                            high_halves(pair + 1, 2, k_hi, bks_col, 0)
                if ahead:
                    for b in range(2):
                        relative_queries(pair + 1, b)
                rel_out(pair, STEPS - 1)

            def pair_steps(pair, ahead):
                step(pair, 0, first=True, rel=False)
                key_window(pair, 1)
                act.wait_ge(rel_stored, START + pair * 16)
                step(pair, 1, rel=False)
                key_window(pair, 2)
                with act.Fori(2, STEPS - 1) as s:
                    step(pair, s)
                    key_window(pair, s + 1)
                step(pair, STEPS - 1)
                if ahead:
                    key_window(pair + 1, 0)
                last_step(pair, ahead)

            key_window(0, 0)
            rows_t(0)
            high_halves(0, 0, q_hi, bq_col, 2)
            high_halves(0, 2, k_hi, bks_col, 0)
            for b in range(2):
                relative_queries(0, b)
            with act.Fori(0, PAIRS - 1) as pair:
                pair_steps(pair, True)
            pair_steps(PAIRS - 1, False)

            def prepare_h(b, slot):
                act.wait_ge(hn_tr, START + b + 1)
                nc.scalar.activation(h_t[:, slot, :], ps[:, 0, :], ACT.Copy).then_inc(h_ready, 1)

            def batch(b, slot, ahead):
                for e in range(EXPERTS):
                    for k in range(2):
                        act.wait_ge(up_done, START + b * 20 + e * 2 + k + 1)
                        act.wait_ge(down_done, START + b * EXPERTS + max(e - 1, 0))
                        nc.scalar.activation(hid[:, e % 2, k, :], ps[:, 4 + k, :], ACT.Gelu, bias=b1_s[:, e, k:k + 1]).then_inc(gelu_done, 1)
                    if ahead and e == 4:
                        prepare_h(b + 1, 1 - slot)
                    if ahead and e == 9:
                        prepare_weights(b + 1)

            def prepare_weights(b):
                act.wait_ge(comb_tr, START + b + 1)
                nc.scalar.activation(comb_t[:], ps[0:EXPERTS, 1, :], ACT.Copy).then_inc(comb_t_ready, 1)

            prepare_h(0, 0)
            prepare_weights(0)
            with act.Fori(0, B // 2 - 1) as i:
                batch(2 * i, 0, True)
                batch(2 * i + 1, 1, True)
            batch(B - 2, 0, True)
            batch(B - 1, 1, False)

        @block.vector
        def _(dve):
            dve.wait_ge(loaded, 16 * LOADS)
            nc.vector.tensor_copy(mask16h[:], const[:, M16:M16 + H]).then_inc(setup_dve, 1)
            nc.vector.tensor_copy(mask8h[:], const[:, M8:M8 + DK]).then_inc(setup_dve, 1)
            nc.vector.tensor_copy(mask4h[:], m4.unsqueeze(2).broadcast_to([P, QT, DK])).then_inc(setup_dve, 1)
            nc.vector.tensor_copy(identh[:], ident).then_inc(setup_dve, 1)
            nc.vector.tensor_copy(rk_split[:], rk3[:]).then_inc(setup_dve, 1)
            nc.vector.tensor_scalar(wk_s[:], wk_s[:], SCALE, None, ALU.mult).then_inc(setup_dve, 1)
            nc.vector.tensor_scalar(bks_col[:], bk_col[:], SCALE, None, ALU.mult).then_inc(setup_dve, 1)
            dve.wait_ge(setup_dve, 7)
            nc.vector.tensor_tensor(rk_split[32:64, :], rk3[32:64, :], rk_split[32:64, :], ALU.subtract).then_inc(setup_dve, 1)
            dve.wait_ge(setup_dve, SETUP_DVE)
            dve.wait_ge(setup_pool, SETUP_POOL)

            class Links:
                def __init__(self, semaphore, before):
                    self.semaphore, self.before, self.n = semaphore, before, 0

                def __call__(self, ins):
                    self.n += 1
                    ins.then_inc(self.semaphore, 1)

                def wait(self):
                    dve.wait_ge(self.semaphore, START + self.before + self.n)

                def settle(self):
                    self.wait()
                    nc.vector.memset(settled[:], 0.0)

            LN_LINKS, SPLIT_LINKS = 9, 4

            def variances(pair):
                link = Links(ln_link, pair * LN_LINKS)
                dve.wait_ge(x_landed, START + (pair + 1) * 16)
                for t in range(8):
                    link(nc.vector.bn_stats(stats[:, t, :], x_pair[:, t, :]))
                link.settle()
                for t in range(8):
                    last = nc.vector.bn_aggr(mv[:, t, :], stats[:, t, :])
                link(last)
                link.wait()
                nc.vector.tensor_scalar(var_eps[:], mv[:, :, 1], LN_EPS, None, ALU.add).then_inc(var_ready, 1)
                assert link.n == LN_LINKS

            def normalised(pair):
                dve.wait_ge(rstd_ready, START + pair + 1)
                for t in range(8):
                    nc.vector.tensor_scalar(xn[:, t, :], x_pair[:, t, :], mv[:, t, 0:1], rstd[:, t:t + 1],
                                            ALU.subtract, ALU.mult).then_inc(xn_ready, 1)

            def low_halves(pair, n, hi, lo, bias, bank):
                for b in range(2):
                    dve.wait_ge(hi_ready, START + pair * 4 + n + b + 1)
                    cols = slice(b * L, (b + 1) * L)
                    nc.vector.scalar_tensor_tensor(lo[:, cols], ps[:, bank + b, :], bias[:, 0:1], hi[:, cols], ALU.add,
                                                   ALU.subtract).then_inc(operands_ready, 1)

            def split_queries(pair):
                link = Links(dve_link, pair * SPLIT_LINKS)
                for b in range(2):
                    dve.wait_ge(proj_done, START + pair * 8 + 5 + b)
                    link(nc.vector.tensor_tensor(q_nat[:, b, :, :], ps[:, 2 + b, :].rearrange("p (l c) -> p l c", l=QT),
                                                 bq_row[:].unsqueeze(1).broadcast_to([P, QT, D]), ALU.add))
                    link.wait()
                    natural = q_nat[:, b, :, :].rearrange("p l (h d) -> p h l d", d=DK)
                    link(nc.vector.tensor_copy(q_split[:, b, :, 0, :, :], natural))
                    link.wait()
                    nc.vector.tensor_copy(q_split[:, b, :, 1, :, :], q_split[:, b, :, 0, :, :]).then_inc(q_split_ready, 1)
                    nc.vector.tensor_tensor(q_split[:, b, :, 2, :, :], natural, q_split[:, b, :, 0, :, :],
                                            ALU.subtract).then_inc(q_split_ready, 1)
                assert link.n == SPLIT_LINKS

            def values(pair):
                for b in range(2):
                    dve.wait_ge(proj_done, START + pair * 8 + 7 + b)
                    nc.vector.tensor_tensor(v_s[:, b * 4:b * 4 + 4, :], ps[:, b, :].rearrange("p (t c) -> p t c", t=RT),
                                            bv_row[:].unsqueeze(1).broadcast_to([P, RT, D]), ALU.add).then_inc(operands_ready, 1)

            def queries(pair, s):
                dve.wait_ge(score_done, START + pair * TILES + s * QUADS)
                rows = q_twice[:].rearrange("p a (b c) -> p (a b) c", b=2)[:, :, bass.ds(s * ROWS, ROWS)]
                nc.vector.tensor_tensor(stat_hi[:].rearrange("p a b q (l h) -> p (a b) (q l) h", h=DK),
                                        rows.unsqueeze(3).broadcast_to([P, 4, ROWS, DK]),
                                        mask8h[:].unsqueeze(1).unsqueeze(1).broadcast_to([P, 4, ROWS, DK]), ALU.mult)
                for b in range(2):
                    for half in range(2):
                        rows = q_lo[:, bass.ds(b * L + s * ROWS, ROWS)].rearrange("p (q l) -> p q l", l=QT)
                        last = nc.vector.tensor_tensor(
                            stat_lo[:, b, :, half, :].rearrange("p q (l h) -> p q l h", l=QT),
                            rows.unsqueeze(3).broadcast_to([P, QUADS, QT, DK]),
                            mask16h[:, half * 8:half * 8 + 8].unsqueeze(1).unsqueeze(1).broadcast_to([P, QUADS, QT, DK]), ALU.mult)
                last.then_inc(stat_ready, 1)

            def evacuate(pair, s, q):
                dve.wait_ge(tr_done, START + pair * TILES + s * QUADS + q + 1)
                nc.vector.tensor_copy(probs_t[:, q, :, :].rearrange("p r c -> p (r c)"), ps[:, 4 + q % 2, :]).then_inc(evac_dve, 1)

            def reciprocal(pair, s, q, first):
                dve.wait_ge(exp_done, START + pair * TILES + s * QUADS + q + 1)
                if not first:
                    dve.wait_ge(norm_done, START + pair * TILES + (s - 1) * QUADS + q + 1)
                nc.vector.reciprocal(inv_sum[:, q:q + 1], row_sum[:, q:q + 1]).then_inc(inv_done, 1)

            STEP_LINKS = 2

            def reduce_products(pair, s):
                link = Links(step_link, (pair * STEPS + s) * STEP_LINKS)
                dve.wait_ge(av_v_done, START + pair * STEPS + s + 1)
                link(nc.vector.tensor_tensor(v_masked[:], ps[:, 6, 0:256].rearrange("p (c h) -> p c h", h=4),
                                             m4.unsqueeze(1).broadcast_to([P, 2 * ROWS, 4]), ALU.mult))
                link.wait()
                for b in range(2):
                    last = nc.vector.tensor_reduce(attn_t[:, bass.ds(pair * TOK + b * L + s * ROWS, ROWS)],
                                                   v_masked[:, b * ROWS:(b + 1) * ROWS, :], op=ALU.add, axis=AX_X)
                last.then_inc(v_red, 1)
                dve.wait_ge(av_r_done, START + pair * STEPS + s + 1)
                link(nc.vector.tensor_tensor(r_masked[:], ps[:, 7, 0:256].rearrange("p (g l h) -> p g l h", l=QT, h=DK),
                                             m4.unsqueeze(1).unsqueeze(3).broadcast_to([P, 8, QT, DK]), ALU.mult))
                link.wait()
                nc.vector.tensor_reduce(rel_o[:].rearrange("p a (g h) -> p (a g) h", h=DK), r_masked[:].rearrange("p g l h -> p g h l"),
                                        op=ALU.add, axis=AX_X).then_inc(r_red, 1)

            def step(pair, s, first=False, more=True):
                for q in range(QUADS):
                    if not first and q in DVE_EVAC:
                        evacuate(pair, s - 1, q)
                    dve.wait_ge(score_done, START + pair * TILES + s * QUADS + q + 1)
                    nc.vector.tensor_reduce(neg_max[:, q:q + 1], ps[:, q % S_BANKS, :], op=ALU.max, axis=AX_X,
                                            negate=True).then_inc(max_done, 1)
                    if q >= LAG:
                        reciprocal(pair, s, q - LAG, first)
                for q in range(QUADS - LAG, QUADS):
                    reciprocal(pair, s, q, first)
                if more:
                    queries(pair, s + 1)

            def first_queries(pair):
                dve.wait_ge(q_twice_landed, START + (pair + 1) * 64)
                queries(pair, 0)

            def last_step(pair, ahead):
                if ahead:
                    normalised(pair + 1)
                evacuate(pair, STEPS - 1, DVE_EVAC[0])
                if ahead:
                    low_halves(pair + 1, 0, q_hi, q_lo, bq_col, 2)
                    low_halves(pair + 1, 2, k_hi, k_lo, bks_col, 0)
                evacuate(pair, STEPS - 1, DVE_EVAC[1])
                if ahead:
                    split_queries(pair + 1)
                    first_queries(pair + 1)
                reduce_products(pair, STEPS - 1)
                if ahead:
                    values(pair + 1)

            def pair_steps(pair, ahead):
                step(pair, 0, first=True)
                with dve.Fori(1, STEPS - 1) as s:
                    step(pair, s)
                    reduce_products(pair, s - 1)
                step(pair, STEPS - 1, more=False)
                if ahead:
                    variances(pair + 1)
                reduce_products(pair, STEPS - 2)
                last_step(pair, ahead)

            variances(0)
            normalised(0)
            low_halves(0, 0, q_hi, q_lo, bq_col, 2)
            low_halves(0, 2, k_hi, k_lo, bks_col, 0)
            split_queries(0)
            first_queries(0)
            values(0)
            with dve.Fori(0, PAIRS - 1) as pair:
                pair_steps(pair, True)
            pair_steps(PAIRS - 1, False)

            FFN_LINKS = 13

            def prepare_attention(b, link):
                dve.wait_ge(rel_nat_tr, START + b + 1)
                nc.vector.tensor_tensor(o_sum_t, ps[:, 0, :], attn_t[:, bass.ds(b * L, L)], ALU.add).then_inc(o_ready, 1)

            def prepare_residual(b, slot, link):
                dve.wait_ge(wo_done, START + b + 1)
                rows = acc[:, slot, :, :]
                dve.wait_ge(x_batch_landed, START + (b + 1) * 16)
                link(nc.vector.tensor_tensor(xn[:, 0:TPB, :], ps[:, 1, :].rearrange("p (t d) -> p t d", t=TPB), x_batch, ALU.add))
                link.wait()
                link(nc.vector.tensor_tensor(rows, xn[:, 0:TPB, :], bo_row[:].unsqueeze(1).broadcast_to([P, TPB, D]), ALU.add))
                link.wait()
                for t in range(TPB):
                    last = nc.vector.bn_stats(stats[:, t, :], acc[:, slot, t, :])
                link(last)
                link.settle()
                for t in range(TPB):
                    last = nc.vector.bn_aggr(mv[:, t, :], stats[:, t, :])
                link(last)
                link.wait()
                nc.vector.tensor_scalar(var_eps[:, 0:TPB], mv[:, 0:TPB, 1], LN_EPS, None, ALU.add).then_inc(x1_var, 1)

            def prepare_norm(b, slot, link):
                dve.wait_ge(x1_rstd, START + b + 1)
                for t in range(TPB):
                    last = nc.vector.tensor_scalar(xn[:, t, :], acc[:, slot, t, :], mv[:, t, 0:1], rstd[:, t:t + 1],
                                                   ALU.subtract, ALU.mult)
                last.then_inc(hn_ready, 1)

            def prepare_gates(b, link):
                dve.wait_ge(gate_done, START + b + 1)
                link(nc.vector.tensor_tensor(gates[:], ps[:, 2, 0:TPB * NE].rearrange("p (t e) -> p t e", t=TPB),
                                             rb_row[:].unsqueeze(1).broadcast_to([P, TPB, NE]), ALU.add))
                link.settle()
                for t in range(TPB):
                    last = nc.vector.max(top8[:, t, :], gates[:, t, :])
                link(last)
                link.settle()
                for t in range(TPB):
                    last = nc.vector.max_index(top_i[:, t, :], top8[:, t, :], gates[:, t, :])
                link(last)
                link.wait()
                link(nc.vector.tensor_copy(top_f[:], top_i[:, :, 0:2]))
                nc.vector.tensor_tensor(gap[:], top8[:, :, 1], top8[:, :, 0], ALU.subtract).then_inc(gap_ready, 1)

            def prepare_comb(b, slot, link):
                dve.wait_ge(e_gap_ready, START + b + 1)
                link(nc.vector.tensor_scalar(prob2[:, :, 1], e_gap[:], 1.0, None, ALU.add))
                link.wait()
                link(nc.vector.reciprocal(prob2[:, :, 0], prob2[:, :, 1]))
                link.wait()
                link(nc.vector.tensor_tensor(prob2[:, :, 1], prob2[:, :, 0], e_gap[:], ALU.mult))
                link.wait()
                for t in range(TPB):
                    for j in range(2):
                        last = nc.vector.tensor_scalar(pick[:, t, j, :], iota8, top_f[:, t, j:j + 1], prob2[:, t, j:j + 1],
                                                       ALU.is_equal, ALU.mult)
                link(last)
                link.wait()
                nc.vector.tensor_tensor(comb[:, slot, :, NS:], pick[:, :, 0, :], pick[:, :, 1, :], ALU.add).then_inc(comb_ready, 1)

            def prepare_bias(b, slot, link):
                dve.wait_ge(bias_done, START + b + 1)
                link(nc.vector.tensor_tensor(acc[:, slot, :, :], ps[:, 3, :].rearrange("p (t d) -> p t d", t=TPB),
                                             acc[:, slot, :, :], ALU.add))
                link.wait()

            def expert(b, slot, e):
                dve.wait_ge(down_done, START + b * EXPERTS + e + 1)
                for t in range(TPB):
                    last = nc.vector.scalar_tensor_tensor(acc[:, slot, t, :], ps[:, 6 + e % 2, t * D:(t + 1) * D],
                                                          comb[:, slot, t, e:e + 1], acc[:, slot, t, :], ALU.mult, ALU.add)
                last.then_inc(final_ready if e == EXPERTS - 1 else y_used, 1)
                if e < EXPERTS - 1:
                    dve.wait_ge(y_used, START + b * (EXPERTS - 1) + e + 1)
                else:
                    dve.wait_ge(final_ready, START + b + 1)

            def batch(b, slot, ahead):
                link = Links(ffn_link, (b + 1) * FFN_LINKS)
                for e in range(EXPERTS):
                    expert(b, slot, e)
                    if ahead:
                        if e == 0:
                            prepare_attention(b + 1, link)
                        if e == 1:
                            dve.wait_ge(stored, START + (b + 1 - 1) * 16)
                            prepare_residual(b + 1, 1 - slot, link)
                        if e == 2:
                            prepare_norm(b + 1, 1 - slot, link)
                        if e == 5:
                            prepare_gates(b + 1, link)
                        if e == 6:
                            prepare_comb(b + 1, 1 - slot, link)
                        if e == 9:
                            prepare_bias(b + 1, 1 - slot, link)
                assert not ahead or link.n == FFN_LINKS, link.n

            link = Links(ffn_link, 0)
            prepare_attention(0, link)
            prepare_residual(0, 0, link)
            prepare_norm(0, 0, link)
            prepare_gates(0, link)
            prepare_comb(0, 0, link)
            prepare_bias(0, 0, link)
            assert link.n == FFN_LINKS, link.n
            with dve.Fori(0, B // 2 - 1) as i:
                batch(2 * i, 0, True)
                batch(2 * i + 1, 1, True)
            batch(B - 2, 0, True)
            batch(B - 1, 1, False)

        @block.tensor
        def _(pe):
            pe.wait_ge(loaded, 16 * LOADS)
            pe.wait_ge(setup_dve, SETUP_DVE)

            def rows_t(pair):
                for half in range(2):
                    pe.wait_ge(xn_ready, START + pair * 8 + half * 4 + 4)
                    for t in range(4):
                        last = nc.tensor.transpose(ps[:, half, t * P:(t + 1) * P], xn[:, half * 4 + t, :], ident)
                    last.then_inc(xn_tr, 1)

            def project(w, bank):
                for b in range(2):
                    nc.tensor.matmul(ps[:, bank + b, :], w[:], xn_t[:, b * L:(b + 1) * L], start=True, stop=True).then_inc(proj_done, 1)

            def project_queries(pair):
                pe.wait_ge(xn_t_ready, START + pair * 2 + 2)
                project(wq_s, 2)

            def project_keys(pair):
                project(wk_s, 0)

            def natural_queries(pair):
                pe.wait_ge(operands_ready, START + pair * 6 + 2)
                for b in range(2):
                    for l in range(QT):
                        rows = xn_t[:, b * L:(b + 1) * L].rearrange("p (q l) -> p l q", l=QT)[:, l, :]
                        last = nc.tensor.matmul(ps[:, 2 + b, l * D:(l + 1) * D], rows, wq_s[:], start=True, stop=True)
                    last.then_inc(proj_done, 1)

            def relative_queries(pair, b):
                if b == 0:
                    pe.wait_ge(operands_ready, START + pair * 6 + 4)
                pe.wait_ge(q_split_ready, START + pair * 4 + b * 2 + 2)
                for half in range(2):
                    for h in range(8):
                        pieces = q_split[:, b, half * 8 + h, :, :, :].rearrange("p a l d -> p (a l d)")
                        last = nc.tensor.transpose(bank_h(b * 2 + half, 8 * P)[0:REL_K, h * P:(h + 1) * P], pieces, identh[:])
                    last.then_inc(q_rel_tr, 1)

            def project_values(pair):
                pe.wait_ge(q_rel_ready, START + pair * 4 + 2)
                for b in range(2):
                    for t in range(RT):
                        last = nc.tensor.matmul(ps[:, b, t * D:(t + 1) * D], xn_t[:, b * L + t * P:b * L + (t + 1) * P], wv_s[:],
                                                start=True, stop=True)
                    last.then_inc(proj_done, 1)

            def operands(pair):
                pe.wait_ge(q_rel_ready, START + pair * 4 + 4)
                pe.wait_ge(operands_ready, START + pair * 6 + 6)
                pe.wait_ge(k_both_landed, START + (pair + 1) * 64)

            def scores(pair, s, q, first):
                if q == 0:
                    pe.wait_ge(stat_ready, START + pair * STEPS + s + 1)
                    pe.wait_ge(stat_rel_ready, START + pair * STEPS + s + 1)
                    pe.wait_ge(rk_landed, START + (pair * STEPS + s + 1) * 16)
                if not (first and q < S_BANKS):
                    pe.wait_ge(exp_done, START + pair * TILES + s * QUADS + q - S_BANKS + 1)
                bank = ps[:, q % S_BANKS, :]
                window = (ROWS - QT) - QT * q
                nc.tensor.matmul(bank, stat_rel[:, q, :, :, :].rearrange("k g l h -> k (g l h)"), rk_step[:, window:window + L],
                                 start=True, stop=False, skip_group_check=True)
                for b in range(2):
                    for half in range(2):
                        at = b * 64 + half * 32
                        nc.tensor.matmul(ps[at:at + 32, q % S_BANKS, :], stat_hi[:, half, b, q, :], k_both[:, half, b * L:(b + 1) * L],
                                         start=False, stop=False, skip_group_check=True)
                for b in range(2):
                    last = nc.tensor.matmul(ps[b * 64:b * 64 + 64, q % S_BANKS, :], stat_lo[:, b, q, :, :].rearrange("p a c -> p (a c)"),
                                            k_hi[:, b * L:(b + 1) * L], start=False, stop=True, skip_group_check=True)
                last.then_inc(score_done, 1)

            def transposes(pair, s, q):
                pe.wait_ge(norm_done, START + pair * TILES + s * QUADS + q + 1)
                if q >= 2:
                    if q - 2 in ACT_EVAC:
                        pe.wait_ge(evac_act, START + (pair * STEPS + s) * len(ACT_EVAC) + ACT_EVAC.index(q - 2) + 1)
                    else:
                        pe.wait_ge(evac_dve, START + (pair * STEPS + s) * len(DVE_EVAC) + DVE_EVAC.index(q - 2) + 1)
                for rt in range(RT):
                    last = nc.tensor.transpose(ps[:, 4 + q % 2, rt * P:(rt + 1) * P], probs[:, q, rt * P:(rt + 1) * P], ident)
                last.then_inc(tr_done, 1)

            def value_products(pair, s):
                pe.wait_ge(evac_act, START + (pair * STEPS + s + 1) * len(ACT_EVAC))
                pe.wait_ge(evac_dve, START + (pair * STEPS + s + 1) * len(DVE_EVAC))
                pe.wait_ge(v_red, START + pair * STEPS + s)
                pe.wait_ge(rel_t_ready, START + pair * STEPS + s)
                for b in range(2):
                    for rt in range(RT):
                        for g in range(4):
                            at = b * 64 + (g // 2) * 32
                            cols = probs_t[:, :, rt, at:at + 32].rearrange("p q (l h) -> p q l h", l=QT)[:, :, :, (g % 2) * 4:(g % 2) * 4 + 4]
                            last = nc.tensor.matmul(ps[32 * g:32 * g + 32, 6, b * P:(b + 1) * P], v_s[:, b * 4 + rt, 32 * g:32 * g + 32], cols,
                                                    start=rt == 0, stop=rt == RT - 1, skip_group_check=True)
                last.then_inc(av_v_done, 1)

            def relative_products(pair, s):
                pe.wait_ge(rv_landed, START + (pair * STEPS + s + 1) * 16)
                pe.wait_ge(r_red, START + pair * STEPS + s)
                for half in range(2):
                    for rt in range(RT):
                        for g in range(4):
                            q = half * 4 + g
                            last = nc.tensor.matmul(ps[32 * g:32 * g + 32, 7, half * P:(half + 1) * P], rv_step[:, RT - 1 - rt, q * 32:q * 32 + 32],
                                                    probs_t[:, q, rt, :], start=rt == 0, stop=rt == RT - 1, skip_group_check=True)
                last.then_inc(av_r_done, 1)

            def rel_transposes(pair, s):
                pe.wait_ge(r_red, START + pair * STEPS + s + 1)
                pe.wait_ge(v_red, START + pair * STEPS + s + 1)
                for half in range(2):
                    last = nc.tensor.transpose(ps[0:32, 6, 256 + half * P:256 + (half + 1) * P], rel_o[:, half, :], ident)
                last.then_inc(rel_tr, 1)

            def step(pair, s, first=False, rel=True):
                for q in range(QUADS):
                    if not first:
                        transposes(pair, s - 1, q)
                    if rel and q == 4:
                        rel_transposes(pair, s - 2)
                    scores(pair, s, q, first)
                if not first:
                    value_products(pair, s - 1)
                    relative_products(pair, s - 1)

            def last_step(pair, ahead):
                s = STEPS - 1
                for q in range(QUADS):
                    transposes(pair, s, q)
                    if q == 4:
                        rel_transposes(pair, s - 1)
                    if ahead:
                        if q == 1:
                            pe.wait_ge(exp_done, START + (pair + 1) * TILES)
                            rows_t(pair + 1)
                        if q == 3:
                            project_queries(pair + 1)
                        if q == 5:
                            project_keys(pair + 1)
                if ahead:
                    natural_queries(pair + 1)
                value_products(pair, s)
                if ahead:
                    pe.wait_ge(q_split_ready, START + (pair + 1) * 4 + 4)
                    relative_queries(pair + 1, 0)
                relative_products(pair, s)
                if ahead:
                    relative_queries(pair + 1, 1)
                rel_transposes(pair, s)
                if ahead:
                    project_values(pair + 1)
                    operands(pair + 1)

            def pair_steps(pair, ahead):
                step(pair, 0, first=True, rel=False)
                step(pair, 1, rel=False)
                with pe.Fori(2, STEPS) as s:
                    step(pair, s)
                last_step(pair, ahead)

            rows_t(0)
            project_queries(0)
            project_keys(0)
            natural_queries(0)
            for b in range(2):
                relative_queries(0, b)
            project_values(0)
            operands(0)
            with pe.Fori(0, PAIRS - 1) as pair:
                pair_steps(pair, True)
            pair_steps(PAIRS - 1, False)
            pe.wait_ge(rel_t_ready, START + PAIRS * STEPS)

            def prepare_attention(b):
                pe.wait_ge(rel_landed, START + (b + 1) * 16 * TPB)
                for t in range(TPB):
                    last = nc.tensor.transpose(ps[:, 0, t * P:(t + 1) * P], rel_nat[:, t, :, :].rearrange("p h d -> p (h d)"), ident)
                last.then_inc(rel_nat_tr, 1)

            def prepare_output(b):
                pe.wait_ge(o_ready, START + b + 1)
                for t in range(TPB):
                    last = nc.tensor.matmul(ps[:, 1, t * D:(t + 1) * D], o_sum_t[:, t * P:(t + 1) * P], wo_s[:], start=True, stop=True)
                last.then_inc(wo_done, 1)

            def prepare_h(b):
                pe.wait_ge(hn_ready, START + b + 1)
                for t in range(TPB):
                    last = nc.tensor.transpose(ps[:, 0, t * P:(t + 1) * P], xn[:, t, :], ident)
                last.then_inc(hn_tr, 1)

            def prepare_gates(b, slot):
                pe.wait_ge(h_ready, START + b + 1)
                for t in range(TPB):
                    last = nc.tensor.matmul(ps[:, 2, t * NE:(t + 1) * NE], h_t[:, slot, t * P:(t + 1) * P], rw_s[:], start=True, stop=True)
                last.then_inc(gate_done, 1)

            def prepare_comb(b, slot):
                pe.wait_ge(comb_ready, START + b + 1)
                for t in range(TPB):
                    last = nc.tensor.transpose(ps[0:EXPERTS, 1, t * P:(t + 1) * P], comb[:, slot, t, :], ident)
                last.then_inc(comb_tr, 1)

            def prepare_bias(b):
                pe.wait_ge(comb_t_ready, START + b + 1)
                for t in range(TPB):
                    last = nc.tensor.matmul(ps[:, 3, t * D:(t + 1) * D], comb_t[:, t * P:(t + 1) * P], b2_s[:], start=True, stop=True)
                last.then_inc(bias_done, 1)

            def up(b, slot, e):
                for k in range(2):
                    pe.wait_ge(gelu_done, START + b * 20 + (e * 2 + k - 1 if e else 0))
                    nc.tensor.matmul(ps[:, 4 + k, :], w1_s[:, e, k * P:(k + 1) * P], h_t[:, slot, :], start=True, stop=True).then_inc(up_done, 1)

            def down(b, e):
                pe.wait_ge(gelu_done, START + b * 20 + e * 2 + 2)
                if e >= 2:
                    pe.wait_ge(y_used, START + b * (EXPERTS - 1) + e - 1)
                else:
                    pe.wait_ge(final_ready, START + b)
                for t in range(TPB):
                    for k in range(2):
                        last = nc.tensor.matmul(ps[:, 6 + e % 2, t * D:(t + 1) * D], hid[:, e % 2, k, t * P:(t + 1) * P], w2_s[:, e, k, :],
                                                start=k == 0, stop=k == 1)
                last.then_inc(down_done, 1)

            def batch(b, slot, ahead):
                up(b, slot, 0)
                for e in range(EXPERTS):
                    if e + 1 < EXPERTS:
                        up(b, slot, e + 1)
                    down(b, e)
                    if ahead:
                        if e == 0:
                            prepare_attention(b + 1)
                        if e == 1:
                            prepare_output(b + 1)
                        if e == 3:
                            prepare_h(b + 1)
                        if e == 4:
                            prepare_gates(b + 1, 1 - slot)
                        if e == 7:
                            prepare_comb(b + 1, 1 - slot)
                        if e == 9:
                            prepare_bias(b + 1)

            prepare_attention(0)
            prepare_output(0)
            prepare_h(0)
            prepare_gates(0, 0)
            prepare_comb(0, 0)
            prepare_bias(0)
            with pe.Fori(0, B // 2 - 1) as i:
                batch(2 * i, 0, True)
                batch(2 * i + 1, 1, True)
            batch(B - 2, 0, True)
            batch(B - 1, 1, False)


def relative_windows(table_k, table_v):
    n = 2 * MAX_LEN - 1

    def at(apart):
        index = apart + MAX_LEN - 1
        return np.clip(np.where(index < 0, index + n, index), 0, n - 1)

    rows, cols = np.arange(QT)[:, None], np.arange(RK_COLS)[None, :]
    keys = table_k[at(cols - (L - QT) - rows)]
    rk = np.ascontiguousarray(keys.transpose(0, 2, 1).reshape(QT * DK, RK_COLS))
    part, cols = np.arange(P)[:, None], np.arange(RV_COLS)[None, :]
    rv = np.ascontiguousarray(table_v[at(part - cols + (L - P))].reshape(P, RV_COLS * DK))
    return rk, rv


def constants():
    row = np.arange(P)[:, None]
    c = np.zeros((P, CONSTS), np.float32)
    c[:, M4:M4 + 4] = (row // DK) % 4 == np.arange(4)[None, :]
    c[:, M16:M16 + H] = row // DK == np.arange(H)[None, :]
    c[:, IOTA:IOTA + NE] = np.arange(NE)[None, :]
    c[:, M8:M8 + DK] = (row // DK) % 8 == np.arange(DK)[None, :]
    c[:, IDENT:] = np.eye(P)
    return c


def kernel(**inputs):
    import concourse.bacc as bacc
    from concourse.bass_utils import run_bass_kernel_spmd

    given = {name: np.asarray(a) for name, a in inputs.items()}
    rk, rv = relative_windows(given["L0_attn_relative_k"], given["L0_attn_relative_v"])
    arrays = {"x": given["L0_attn_x"].reshape(B * L, D)}
    for name in ("Wq", "Wk", "Wv", "Wo"):
        arrays[name.lower() + "_t"] = given["L0_attn_" + name].T
    for name in ("bq", "bk", "bv", "bo"):
        arrays[name] = given["L0_attn_" + name]
    arrays |= {"rk_win": rk, "rv_win": rv}
    for name, short in (("router_w", "rw"), ("router_b", "rb"), ("w1", "w1"), ("w2", "w2"), ("b2", "b2"),
                        ("sw1", "sw1"), ("sw2", "sw2"), ("sb2", "sb2")):
        arrays[short] = given["L0_ffn_" + name]
    b1 = np.concatenate([given["L0_ffn_sb1"], given["L0_ffn_b1"]])
    arrays["b1_cols"] = b1.reshape(EXPERTS, 2, P).transpose(2, 0, 1)
    arrays["consts"] = constants()

    nc = bacc.Bacc("TRN2", target_bir_lowering=False, num_devices=1)
    args, in_map = [], {}
    for name, a in arrays.items():
        a = np.ascontiguousarray(a)
        in_map["in_" + name] = a
        args.append(nc.dram_tensor("in_" + name, a.shape, mybir.dt.from_np(a.dtype), kind="ExternalInput").ap())
    args.append(nc.dram_tensor("rel_scratch", (B * H, L * DK), F32, kind="Internal").ap())
    args.append(nc.dram_tensor("out", (B * L, D), F32, kind="ExternalOutput").ap())
    attention_ffn(nc, *args)
    r = run_bass_kernel_spmd(nc, [in_map], core_ids=[0])
    return r.results[0]["out"].reshape(B, L, D)
```

```python
import math
from contextlib import ExitStack

import numpy as np

import concourse.bass as bass
from concourse import mybir

F32 = mybir.dt.float32
F16 = mybir.dt.float16
U32 = mybir.dt.uint32
U8 = mybir.dt.uint8
ALU = mybir.AluOpType
ACT = mybir.ActivationFunctionType
AX_X = mybir.AxisListType.X

P = 128
B, L, D = 16, 512, 128
H, DK = 16, 8
MAX_LEN = 128
NE, NS, HID = 8, 2, 256
EXPERTS = NS + NE
LN_EPS = 1e-5
SCALE = float(np.float32(1.0) / np.sqrt(DK).astype(np.float32))

PAIRS = B // 2
TOK = 2 * L
QT = 4
QUADS = 8
ROWS = QT * QUADS
STEPS = L // ROWS
RT = L // P
TILES = STEPS * QUADS
REL_K = 3 * QT * DK
WIN = L + ROWS - QT
RK_COLS = 2 * L - QT
RV_COLS = (L - ROWS) + L
TPB = L // P
S_BANKS = 4
GROUPS = L // P
GROUP_STEPS = P // ROWS
FAR = 2
FAR_COLS = (RT - FAR) * P
KEYS = L + FAR_COLS
NEAR_GROUP = RT - FAR
START = 1
W_SCALE = 64.0
LOOK = 2
SLOTS = 4
LAG = 2
ACT_EVAC = (0, 1, 2, 4, 5, 6)
DVE_EVAC = (3, 7)
M4, M16, IOTA, M8 = 0, 4, 20, 28
IDENT = 36
CONSTS = IDENT + P


def attention_ffn(nc, x, w_qkv, cols, rows, wo_t, bo, rk_win, rv_win, rw, rb, w1, w2, b2,
                  sw1, sw2, sb2, b1_cols, consts, rel_scratch, out):
    with ExitStack() as ctx:
        def sb(name, shape, dt=F32):
            return ctx.enter_context(nc.sbuf_tensor(name, shape, dt))

        def sem(name):
            return ctx.enter_context(nc.semaphore(name))

        ps = ctx.enter_context(nc.psum_tensor("ps", [P, 8, 512], F32))

        x_pair = sb("x_pair", [P, 8, D])
        x_batch = x_pair[:, 0:TPB, :]
        attn_t = sb("attn_t", [P, B * L])
        const = sb("const", [P, CONSTS])
        m4, iota8, ident = const[:, M4:M4 + 4], const[:, IOTA:IOTA + NE], const[:, IDENT:IDENT + P]
        mask16h = sb("mask16h", [P, H], F16)
        mask8h = sb("mask8h", [P, DK], F16)
        mask4h = sb("mask4h", [P, QT, DK], F16)
        identh = sb("identh", [P, P], F16)
        w_qkv_s = sb("w_qkv_s", [P, 3, D])
        wq_s, wk_s, wv_s = (w_qkv_s[:, i, :] for i in range(3))
        wo_s = sb("wo_s", [P, D])
        cols_s, rows_s = sb("cols_s", [P, 3]), sb("rows_s", [P, 3, D])
        bq_col, bk_col, rk_last_col = (cols_s[:, i:i + 1] for i in range(3))
        bq_row, bv_row, rv_last_row = (rows_s[:, i, :] for i in range(3))
        bks_col, bk_far_col = sb("bks_col", [P, 1]), sb("bk_far_col", [P, 1])
        bo_row = sb("bo_row", [P, D])
        rk_split = sb("rk_split", [REL_K, RK_COLS], F16)
        rw_s = sb("rw_s", [P, NE])
        rb_row = sb("rb_row", [P, NE])
        w1_s = sb("w1_s", [P, EXPERTS, HID])
        w2_s = sb("w2_s", [P, EXPERTS, 2, D])
        w1_h, w1_l = (sb(n, [P, EXPERTS, HID], F16) for n in ("w1_h", "w1_l"))
        w2_h, w2_l = (sb(n, [P, EXPERTS, 2, D], F16) for n in ("w2_h", "w2_l"))
        b1_s = sb("b1_s", [P, EXPERTS, 2])
        b2_s = sb("b2_s", [EXPERTS, D])
        half_pow = sb("half_pow", [P, 8])
        e_const = sb("e_const", [P, TPB])

        settled = sb("settled", [P, 1])
        stats = sb("stats", [P, 8, 6])
        mv = sb("mv", [P, 8, 2])
        var_eps = sb("var_eps", [P, 8])
        rstd = sb("rstd", [P, 8])
        xn = sb("xn", [P, 8, D])
        xn_t = sb("xn_t", [P, TOK])
        q_hi, q_lo = (sb(n, [P, TOK], F16) for n in ("q_hi", "q_lo"))
        k_hi, k_lo = (sb(n, [P, 2, KEYS], F16) for n in ("k_hi", "k_lo"))
        q_twice = sb("q_twice", [P, 2, TOK], F16)
        k_both = sb("k_both", [P, 2, 2, KEYS], F16)
        v_s = sb("v_s", [P, 8, D])
        v_far = sb("v_far", [P, 2, RT - FAR, D])
        q_nat = sb("q_nat", [P, 2, QT, D])
        q_split = sb("q_split", [P, 2, H, 3, QT, DK], F16)
        q_rel = sb("q_rel", [REL_K, P, 4, DK], F16)

        odd_stat = xn[:].rearrange("p t d -> p (t d)").bitcast(F16).rearrange("p (n c) -> p n c", n=2)
        stat_hi = (sb("stat_hi", [P, 2, 2, QUADS, ROWS], F16),
                   odd_stat[:, 0].rearrange("p (a b q c) -> p a b q c", a=2, b=2, q=QUADS))
        stat_lo = (sb("stat_lo", [P, 2, QUADS, 2, ROWS], F16),
                   odd_stat[:, 1].rearrange("p (b q a c) -> p b q a c", b=2, q=QUADS, a=2))
        odd_rel = q_nat[0:REL_K].rearrange("p b l c -> p (b l c)").bitcast(F16)[:, 0:QUADS * P]
        stat_rel = (sb("stat_rel", [REL_K, QUADS, 4, QT, DK], F16),
                    odd_rel.rearrange("k (q g l h) -> k q g l h", q=QUADS, g=4, l=QT))
        rk_step = sb("rk_step", [REL_K, 2, WIN], F16)
        rv_step = sb("rv_step", [P, RT, ROWS * DK])
        neg_max = sb("neg_max", [P, QUADS])
        row_sum = sb("row_sum", [P, QUADS])
        inv_sum = sb("inv_sum", [P, QUADS])
        probs = sb("probs", [P, QUADS, L])
        rk3 = probs[0:REL_K, 0:2, :].rearrange("p a c -> p (a c)")[:, 0:RK_COLS]
        probs_t = sb("probs_t", [P, QUADS, RT, P])
        v_masked = sb("v_masked", [P, 2 * ROWS, 4])
        r_masked = sb("r_masked", [P, 8, QT, DK])
        rel_o = sb("rel_o", [P, 2, 32])
        rel_t = sb("rel_t", [32, STEPS, 2, P])

        rel_nat = x_pair[:, TPB:2 * TPB, :].rearrange("p t (h d) -> p t h d", h=H)
        o_sum_t = xn_t[:, 0:L]
        h_t = q_nat[:].rearrange("p b l c -> p b (l c)")
        gates = sb("gates", [P, TPB, NE])
        top8 = sb("top8", [P, TPB, 8])
        top_i = sb("top_i", [P, TPB, 8], U32)
        top_f = sb("top_f", [P, TPB, 2])
        gap = sb("gap", [P, TPB])
        e_gap = sb("e_gap", [P, TPB])
        prob2 = sb("prob2", [P, TPB, 2])
        pick = sb("pick", [P, TPB, 2, NE])
        comb = sb("comb", [P, 2, TPB, EXPERTS])
        comb_t = sb("comb_t", [EXPERTS, L])
        acc = sb("acc", [P, 2, TPB, D])
        split = q_split[:].rearrange("p b h a l d -> p (b h a l d)")[:, 0:4 * L].rearrange("p (a s c) -> p a s c", a=2, s=2)
        h_hi, h_lo = split[:, 0], split[:, 1]
        halves = probs_t[:].rearrange("p q r c -> p (q r c)").bitcast(F16).rearrange("p (a s k c) -> p a s k c", a=2, s=SLOTS, k=2)
        hid_h, hid_l = halves[:, 0], halves[:, 1]
        hid = probs[:, 0:4, :].rearrange("p (e k) c -> p e k c", e=2)

        loaded, ffn_loaded = sem("loaded"), sem("ffn_loaded")
        w_high, w_low = sem("w_high"), sem("w_low")
        setup_dve = sem("setup_dve")
        setup_pool = sem("setup_pool")
        x_landed, q_twice_landed, k_both_landed = sem("x_landed"), sem("q_twice_landed"), sem("k_both_landed")
        x_batch_landed = sem("x_batch_landed")
        var_ready, rstd_ready, xn_ready, xn_tr = sem("var_ready"), sem("rstd_ready"), sem("xn_ready"), sem("xn_tr")
        xn_t_ready, proj_done, hi_ready = sem("xn_t_ready"), sem("proj_done"), sem("hi_ready")
        dve_link, ln_link = sem("dve_link"), sem("ln_link")
        operands_ready, q_split_ready, q_rel_tr = sem("operands_ready"), sem("q_split_ready"), sem("q_rel_tr")
        q_rel_ready = sem("q_rel_ready")
        stat_ready, stat_first_odd, stat_rel_ready = sem("stat_ready"), sem("stat_first_odd"), sem("stat_rel_ready")
        rk_landed, rv_landed = (sem("rk_landed_even"), sem("rk_landed_odd")), sem("rv_landed")
        score_done, max_done, exp_done, inv_done = sem("score_done"), sem("max_done"), sem("exp_done"), sem("inv_done")
        norm_done, tr_done, evac_act, evac_dve = sem("norm_done"), sem("tr_done"), sem("evac_act"), sem("evac_dve")
        av_v_done, av_r_done, v_red, r_red = sem("av_v_done"), sem("av_r_done"), sem("v_red"), sem("r_red")
        step_link = sem("step_link")
        rel_tr, rel_t_ready, rel_stored = sem("rel_tr"), sem("rel_t_ready"), sem("rel_stored")
        rel_landed, rel_nat_tr, o_ready, wo_done = sem("rel_landed"), sem("rel_nat_tr"), sem("o_ready"), sem("wo_done")
        ffn_link, x1_var, x1_rstd = sem("ffn_link"), sem("x1_var"), sem("x1_rstd")
        hn_ready, hn_tr, h_ready = sem("hn_ready"), sem("hn_tr"), sem("h_ready")
        h_low, hid_high, hid_low = sem("h_low"), sem("hid_high"), sem("hid_low")
        gate_done, gap_ready, e_gap_ready, comb_ready = sem("gate_done"), sem("gap_ready"), sem("e_gap_ready"), sem("comb_ready")
        comb_tr, comb_t_ready, bias_done, bias_added = sem("comb_tr"), sem("comb_t_ready"), sem("bias_done"), sem("bias_added")
        up_done, gelu_done, down_done, y_used = sem("up_done"), sem("gelu_done"), sem("down_done"), sem("y_used")
        final_ready, stored = sem("final_ready"), sem("stored")

        LOADS = 5
        FFN_LOADS = 13
        SETUP_DVE = 10
        SETUP_POOL = 3

        counted = (av_r_done, av_v_done, bias_added, bias_done, comb_ready, comb_t_ready, comb_tr, dve_link,
                   e_gap_ready, evac_act, evac_dve, exp_done, ffn_link, final_ready, gap_ready, gate_done,
                   gelu_done, h_low, h_ready, hi_ready, hid_high, hn_ready, hn_tr, inv_done, k_both_landed,
                   ln_link, max_done, norm_done, o_ready, operands_ready, proj_done, q_rel_ready, q_rel_tr,
                   q_split_ready, q_twice_landed, r_red, rel_landed, rel_nat_tr, rel_stored, rel_t_ready,
                   rel_tr, *rk_landed, rstd_ready, rv_landed, score_done, stat_first_odd, stat_ready,
                   stat_rel_ready, step_link, stored, tr_done, up_done, v_red, var_ready, wo_done, x1_rstd,
                   x1_var, x_batch_landed, xn_ready, xn_t_ready, xn_tr, y_used)
        counted_back = (down_done, hid_low)

        block = ctx.enter_context(nc.Block())

        def bank_h(bank, n):
            return ps[:, bank, :].bitcast(F16)[:, 0:n]

        def spread_queries(engine, s, odd):
            rows = q_twice[:].rearrange("p a (b c) -> p (a b) c", b=2)[:, :, bass.ds(s * ROWS, ROWS)]
            engine.tensor_tensor(stat_hi[odd][:].rearrange("p a b q (l h) -> p (a b) (q l) h", h=DK),
                                 rows.unsqueeze(3).broadcast_to([P, 4, ROWS, DK]),
                                 mask8h[:].unsqueeze(1).unsqueeze(1).broadcast_to([P, 4, ROWS, DK]), ALU.mult)
            for b in range(2):
                for half in range(2):
                    rows = q_lo[:, bass.ds(b * L + s * ROWS, ROWS)].rearrange("p (q l) -> p q l", l=QT)
                    last = engine.tensor_tensor(
                        stat_lo[odd][:, b, :, half, :].rearrange("p q (l h) -> p q l h", l=QT),
                        rows.unsqueeze(3).broadcast_to([P, QUADS, QT, DK]),
                        mask16h[:, half * 8:half * 8 + 8].unsqueeze(1).unsqueeze(1).broadcast_to([P, QUADS, QT, DK]), ALU.mult)
            return last

        @block.sync
        def _(sp):
            def load(dst, src):
                sp.dma_start(dst, src).then_inc(loaded, 16)

            def load_ffn(dst, src):
                sp.dma_start(dst, src).then_inc(ffn_loaded, 16)

            x_rows = x.rearrange("(n t p) d -> n p t d", t=8, p=P)
            sp.dma_start(x_pair[:], x_rows[0, :, :, :]).then_inc(x_landed, 16)
            load(const[:], consts)
            load(w_qkv_s[:], w_qkv)
            load(cols_s[:], cols)
            load(rows_s[:].rearrange("p a d -> p (a d)"), rows.partition_broadcast(P))
            load(rk3, rk_win)
            for semaphore in counted:
                sp.sem_inc(semaphore, START)
            for semaphore in counted_back:
                sp.sem_inc(semaphore, SLOTS)
            sp.sem_inc(x_landed, START)

            load_ffn(wo_s[:], wo_t)
            load_ffn(rw_s[:], rw)
            for dst, src in ((bo_row, bo), (rb_row, rb)):
                load_ffn(dst[:], src.partition_broadcast(P))
            load_ffn(w1_s[:, 0:NS, :], sw1.rearrange("e d h -> d e h"))
            load_ffn(w1_s[:, NS:, :], w1.rearrange("e d h -> d e h"))
            for k in range(2):
                load_ffn(w2_s[:, 0:NS, k, :], sw2[:, k * P:(k + 1) * P, :].rearrange("e h d -> h e d"))
                load_ffn(w2_s[:, NS:, k, :], w2[:, k * P:(k + 1) * P, :].rearrange("e h d -> h e d"))
            load_ffn(b1_s[:], b1_cols)
            load_ffn(b2_s[0:NS, :], sb2)
            load_ffn(b2_s[NS:, :], b2)

            def value_window(s, multiplied):
                at = sp.snap(sp.to_reg(ROWS * DK * 4 * s))
                blocks = rv_win.bitcast(U8)[:, bass.ds(at, RT * P * DK * 4)].rearrange("p (t c) -> p t c", t=RT)
                sp.wait_ge(av_r_done, START + multiplied)
                sp.dma_start(rv_step[:].bitcast(U8), blocks[:, :, 0:ROWS * DK * 4]).then_inc(rv_landed, 16)

            def double(pair):
                sp.wait_ge(hi_ready, START + pair * 4 + 2)
                for half in range(2):
                    for copy in range(2):
                        sp.dma_start(q_twice[64 * copy:64 * copy + 64, half, :], q_hi[64 * half:64 * half + 64, :]).then_inc(q_twice_landed, 16)
                sp.wait_ge(hi_ready, START + pair * 4 + 4)
                sp.wait_ge(operands_ready, START + pair * 6 + 4)
                for half in range(2):
                    for piece, keys in enumerate((k_hi, k_lo)):
                        sp.dma_start(k_both[64 * piece:64 * piece + 64, half, :, :], keys[64 * half:64 * half + 64, :, :]).then_inc(k_both_landed, 16)

            def pair_windows(pair, ahead):
                with sp.Fori(0, STEPS) as s:
                    value_window(s, pair * STEPS + s)
                if ahead:
                    double(pair + 1)
                row = sp.snap(sp.to_reg(pair * 32))
                sp.wait_ge(rel_t_ready, START + (pair + 1) * STEPS)
                sp.dma_start(rel_scratch[bass.ds(row, 32), :], rel_t[:].rearrange("p s a c -> p (s a c)")).then_inc(rel_stored, 16)

            def next_rows(pair):
                following = sp.snap(sp.to_reg(pair + 1))
                sp.wait_ge(xn_ready, START + pair * 8 + 8)
                sp.dma_start(x_pair[:], x_rows[bass.ds(following, 1), :, :, :].rearrange("n p t d -> (n p) t d")).then_inc(x_landed, 16)

            rel_rows = rel_scratch.rearrange("(b h) (t p d) -> b t p h d", h=H, p=P, d=DK)

            batch_rows = x.rearrange("(n t p) d -> n p t d", t=TPB, p=P)

            def load_rel(b):
                sp.dma_start(x_batch, batch_rows[bass.ds(b, 1), :, :, :].rearrange("n p t d -> (n p) t d")).then_inc(x_batch_landed, 16)
                for t in range(TPB):
                    sp.dma_start(rel_nat[:, t, :, :], rel_rows[bass.ds(b, 1), t, :, :, :].rearrange("b p h d -> (b p) h d")).then_inc(rel_landed, 16)

            out_rows = out.rearrange("(b t p) d -> b p t d", t=TPB, p=P)

            def store(b, slot):
                b = sp.snap(sp.to_reg(b))
                sp.wait_ge(final_ready, START + b + 1)
                sp.dma_start(out_rows[bass.ds(b, 1), :, :, :].rearrange("b p t d -> (b p) t d"), acc[:, slot, :, :]).then_inc(stored, 16)

            def load_next(b):
                sp.wait_ge(rel_nat_tr, START + b)
                sp.wait_ge(x1_var, START + b)
                load_rel(b)

            double(0)
            with sp.Fori(0, PAIRS - 1) as pair:
                next_rows(pair)
                pair_windows(pair, True)
            sp.wait_ge(xn_ready, START + PAIRS * 8)
            sp.wait_ge(rel_stored, START + (PAIRS - 1) * 16)
            load_rel(0)
            pair_windows(PAIRS - 1, False)
            sp.wait_ge(rel_stored, START + PAIRS * 16)
            load_next(1)
            with sp.Fori(0, B // 2 - 1) as i:
                for slot in range(2):
                    load_next(sp.snap(sp.to_reg(2 * i + slot + 2)))
                    store(2 * i + slot, slot)
            store(B - 2, 0)
            store(B - 1, 1)
            sp.wait_ge(stored, START + 16 * B)

        @block.gpsimd
        def _(pool):
            nc.gpsimd.memset(half_pow[:], -0.5).then_inc(setup_pool, 1)
            nc.gpsimd.memset(e_const[:], math.e).then_inc(setup_pool, 1)
            nc.gpsimd.memset(comb[:], 1.0 / NS / W_SCALE).then_inc(setup_pool, 1)
            pool.wait_ge(setup_pool, SETUP_POOL)

            def spread(s, odd):
                quads = q_rel[:, bass.ds(s * QUADS, QUADS), :, :].rearrange("k q g h -> k (q g) h")
                nc.gpsimd.tensor_tensor(
                    stat_rel[odd][:].rearrange("k q g l h -> k (q g) l h"),
                    quads.unsqueeze(2).broadcast_to([REL_K, QUADS * 4, QT, DK]),
                    mask4h[0:REL_K].unsqueeze(1).broadcast_to([REL_K, QUADS * 4, QT, DK]), ALU.mult).then_inc(stat_rel_ready, 1)

            def relative_queries(pair, s, odd):
                pool.wait_ge(score_done, START + pair * TILES + (s - 1) * QUADS)
                spread(s, odd)

            def normalise(done, q):
                pool.wait_ge(inv_done, START + done + q + 1)
                nc.gpsimd.tensor_tensor(probs[:, q, :], probs[:, q, :], inv_sum[:, q:q + 1].broadcast_to([P, L]),
                                        ALU.mult).then_inc(norm_done, 1)

            def deviations(pair):
                pool.wait_ge(var_ready, START + pair + 1)
                nc.gpsimd.tensor_tensor(rstd[:], var_eps[:], half_pow[:], ALU.pow).then_inc(rstd_ready, 1)

            def pair_steps(pair, ahead):
                pool.wait_ge(q_twice_landed, START + (pair + 1) * 64)
                pool.wait_ge(operands_ready, START + pair * 6 + 2)
                spread_queries(nc.gpsimd, 1, 1).then_inc(stat_first_odd, 1)
                for n in range(4):
                    pool.wait_ge(q_rel_ready, START + pair * 4 + n + 1)
                    last = nc.gpsimd.tensor_tensor(
                        stat_rel[0][:, :, n, :, :], q_rel[:, 0:QUADS, n, :].unsqueeze(2).broadcast_to([REL_K, QUADS, QT, DK]),
                        mask4h[0:REL_K].unsqueeze(1).broadcast_to([REL_K, QUADS, QT, DK]), ALU.mult)
                last.then_inc(stat_rel_ready, 1)

                def step(s, odd, more=True):
                    if more:
                        relative_queries(pair, s + 1, 1 - odd)
                    for q in range(QUADS):
                        normalise(pair * TILES + s * QUADS, q)

                with pool.Fori(0, STEPS // 2 - 1) as i:
                    step(2 * i, 0)
                    step(2 * i + 1, 1)
                step(STEPS - 2, 0)
                if ahead:
                    deviations(pair + 1)
                step(STEPS - 1, 1, more=False)

            deviations(0)
            pool.wait_ge(setup_dve, SETUP_DVE)
            with pool.Fori(0, PAIRS - 1) as pair:
                pair_steps(pair, True)
            pair_steps(PAIRS - 1, False)

            def deviations_after(b):
                pool.wait_ge(x1_var, START + b + 1)
                nc.gpsimd.tensor_tensor(rstd[:, 0:TPB], var_eps[:, 0:TPB], half_pow[:, 0:TPB], ALU.pow).then_inc(x1_rstd, 1)

            def gate_exponentials(b):
                pool.wait_ge(gap_ready, START + b + 1)
                nc.gpsimd.tensor_tensor(e_gap[:], e_const[:], gap[:], ALU.pow).then_inc(e_gap_ready, 1)

            def low_rows(b, slot, e):
                pool.wait_ge(hid_high, START + b * EXPERTS + e + 1)
                n = slot * EXPERTS + e
                nc.gpsimd.tensor_tensor(hid_l[:, n % SLOTS, :, :], hid[:, n % 2, :, :], hid_h[:, n % SLOTS, :, :],
                                        ALU.subtract).then_inc(hid_low, 1)

            def batch(b, slot, ahead):
                for e in range(EXPERTS):
                    low_rows(b, slot, e)
                    if ahead and e == 3:
                        deviations_after(b + 1)
                    if ahead and e == 7:
                        gate_exponentials(b + 1)

            deviations_after(0)
            gate_exponentials(0)
            with pool.Fori(0, B // 2 - 1) as i:
                batch(2 * i, 0, True)
                batch(2 * i + 1, 1, True)
            batch(B - 2, 0, True)
            batch(B - 1, 1, False)

        @block.scalar
        def _(act):

            def rows_t(pair):
                for half in range(2):
                    act.wait_ge(xn_tr, START + pair * 2 + half + 1)
                    nc.scalar.activation(xn_t[:, half * L:(half + 1) * L], ps[:, half, :], ACT.Copy).then_inc(xn_t_ready, 1)

            def high_queries(pair):
                for b in range(2):
                    act.wait_ge(proj_done, START + pair * 8 + b + 1)
                    nc.scalar.activation(q_hi[:, b * L:(b + 1) * L], ps[:, 2 + b, :], ACT.Identity,
                                         bias=bq_col[:, 0:1]).then_inc(hi_ready, 1)

            def high_keys(pair):
                for b in range(2):
                    act.wait_ge(proj_done, START + pair * 8 + 2 + b + 1)
                    nc.scalar.activation(k_hi[:, b, 0:L], ps[:, b, :], ACT.Identity, bias=bks_col[:, 0:1])
                    nc.scalar.activation(k_hi[:, b, L:KEYS], ps[:, b, FAR * P:L], ACT.Identity, bias=bk_far_col[:, 0:1]).then_inc(hi_ready, 1)

            def relative_queries(pair, b):
                for half in range(2):
                    n = b * 2 + half
                    act.wait_ge(q_rel_tr, START + pair * 4 + n + 1)
                    nc.scalar.activation(q_rel[:, :, n, :], bank_h(n, 8 * P)[0:REL_K, :].rearrange("k (h q) -> k q h", h=DK),
                                         ACT.Copy).then_inc(q_rel_ready, 1)

            def key_window(pair, s, odd, first=False):
                if not first:
                    act.wait_ge(score_done, START + pair * TILES + (s - 1) * QUADS)
                act.dma_start(rk_step[:, odd, :], rk_split[:, bass.ds(L - ROWS - ROWS * s, WIN)]).then_inc(rk_landed[odd], 16)

            def evacuate(pair, s, q):
                act.wait_ge(tr_done, START + pair * TILES + s * QUADS + q + 1)
                nc.scalar.activation(probs_t[:, q, :, :].rearrange("p r c -> p (r c)"), ps[:, 4 + q % 2, :], ACT.Copy).then_inc(evac_act, 1)

            def exponentials(pair, s, q, first):
                act.wait_ge(max_done, START + pair * TILES + s * QUADS + q + 1)
                if not first:
                    act.wait_ge(tr_done, START + pair * TILES + (s - 1) * QUADS + q + 1)
                nc.scalar.activation(probs[:, q, :], ps[:, q % S_BANKS, :], ACT.Exp, bias=neg_max[:, q:q + 1],
                                     accum_out=row_sum[:, q:q + 1]).then_inc(exp_done, 1)

            def rel_out(pair, s):
                act.wait_ge(rel_tr, START + pair * STEPS + s + 1)
                nc.scalar.activation(rel_t[:, bass.ds(s, 1), :, :].rearrange("p s a c -> p (s a c)"), ps[0:32, 6, 256:512],
                                     ACT.Copy).then_inc(rel_t_ready, 1)

            def step(pair, s, odd, first=False, rel=True, more=True):
                if more:
                    key_window(pair, s + 1, 1 - odd)
                if not first and 0 in ACT_EVAC:
                    evacuate(pair, s - 1, 0)
                for q in range(QUADS):
                    if not first and q + 1 in ACT_EVAC:
                        evacuate(pair, s - 1, q + 1)
                    if rel and q == 5:
                        rel_out(pair, s - 2)
                    if q:
                        exponentials(pair, s, q - 1, first)
                exponentials(pair, s, QUADS - 1, first)

            def last_step(pair, ahead):
                for q in range(QUADS):
                    if q in ACT_EVAC:
                        evacuate(pair, STEPS - 1, q)
                    if q == 5:
                        rel_out(pair, STEPS - 2)
                    if ahead:
                        if q == 1:
                            rows_t(pair + 1)
                        if q == 3:
                            high_queries(pair + 1)
                        if q == 5:
                            high_keys(pair + 1)
                if ahead:
                    for b in range(2):
                        relative_queries(pair + 1, b)
                else:
                    prepare_h(0, 0)
                rel_out(pair, STEPS - 1)

            def high_weights(high, weights):
                nc.scalar.activation(high[:], weights[:], ACT.Copy, scale=W_SCALE).then_inc(w_high, 1)

            def pair_steps(pair, ahead):
                step(pair, 0, 0, first=True, rel=False)
                act.wait_ge(rel_stored, START + pair * 16)
                step(pair, 1, 1, rel=False)
                with act.Fori(1, STEPS // 2 - 1) as i:
                    step(pair, 2 * i, 0)
                    step(pair, 2 * i + 1, 1)
                step(pair, STEPS - 2, 0)
                if ahead:
                    key_window(pair + 1, 0, 0)
                else:
                    act.wait_ge(ffn_loaded, 16 * FFN_LOADS)
                    high_weights(w1_h, w1_s)
                step(pair, STEPS - 1, 1, more=False)
                if not ahead:
                    high_weights(w2_h, w2_s)
                last_step(pair, ahead)

            def prepare_h(b, slot):
                act.wait_ge(hn_tr, START + b + 1)
                nc.scalar.activation(h_t[:, slot, :], ps[:, 0, :], ACT.Copy).then_inc(h_ready, 1)
                nc.scalar.activation(h_hi[:, slot, :], ps[:, 0, :], ACT.Copy).then_inc(h_ready, 1)

            def hidden(b, slot, e):
                n = slot * EXPERTS + e
                act.wait_ge(hid_low, SLOTS + b * EXPERTS + e - 1)
                for k in range(2):
                    act.wait_ge(up_done, START + b * 20 + e * 2 + k + 1)
                    nc.scalar.activation(hid[:, n % 2, k, :], ps[:, 4 + k, :], ACT.Gelu, bias=b1_s[:, e, k:k + 1],
                                         scale=1.0 / W_SCALE).then_inc(gelu_done, 1)
                act.wait_ge(down_done, SLOTS + b * EXPERTS + e - SLOTS + 1)
                act.wait_ge(gelu_done, START + b * 20 + e * 2 + 2)
                nc.scalar.activation(hid_h[:, n % SLOTS, :, :], hid[:, n % 2, :, :], ACT.Copy).then_inc(hid_high, 1)

            def batch(b, slot, ahead):
                for e in range(EXPERTS):
                    hidden(b, slot, e)
                    if e == 1:
                        prepare_weights(b)
                    if ahead and e == 6:
                        prepare_h(b + 1, 1 - slot)

            def prepare_weights(b):
                act.wait_ge(comb_tr, START + b + 1)
                nc.scalar.activation(comb_t[:], ps[0:EXPERTS, 2, :], ACT.Copy).then_inc(comb_t_ready, 1)

            rows_t(0)
            act.wait_ge(loaded, 16 * LOADS)
            act.wait_ge(setup_dve, SETUP_DVE)
            key_window(0, 0, 0, first=True)
            high_queries(0)
            high_keys(0)
            for b in range(2):
                relative_queries(0, b)
            with act.Fori(0, PAIRS - 1) as pair:
                pair_steps(pair, True)
            pair_steps(PAIRS - 1, False)
            with act.Fori(0, B // 2 - 1) as i:
                batch(2 * i, 0, True)
                batch(2 * i + 1, 1, True)
            batch(B - 2, 0, True)
            batch(B - 1, 1, False)

        @block.vector
        def _(dve):
            class Links:
                def __init__(self, semaphore, before):
                    self.semaphore, self.before, self.n = semaphore, before, 0

                def __call__(self, ins):
                    self.n += 1
                    ins.then_inc(self.semaphore, 1)

                def wait(self):
                    dve.wait_ge(self.semaphore, START + self.before + self.n)

                def settle(self):
                    self.wait()
                    nc.vector.memset(settled[:], 0.0)

            LN_LINKS, SPLIT_LINKS = 9, 4

            def variances(pair):
                link = Links(ln_link, pair * LN_LINKS)
                dve.wait_ge(x_landed, START + (pair + 1) * 16)
                for t in range(8):
                    link(nc.vector.bn_stats(stats[:, t, :], x_pair[:, t, :]))
                link.settle()
                for t in range(8):
                    last = nc.vector.bn_aggr(mv[:, t, :], stats[:, t, :])
                link(last)
                link.wait()
                nc.vector.tensor_scalar(var_eps[:], mv[:, :, 1], LN_EPS, None, ALU.add).then_inc(var_ready, 1)
                assert link.n == LN_LINKS

            def normalised(pair):
                dve.wait_ge(rstd_ready, START + pair + 1)
                for t in range(8):
                    nc.vector.tensor_scalar(xn[:, t, :], x_pair[:, t, :], mv[:, t, 0:1], rstd[:, t:t + 1],
                                            ALU.subtract, ALU.mult).then_inc(xn_ready, 1)

            def low_queries(pair):
                for b in range(2):
                    dve.wait_ge(hi_ready, START + pair * 4 + b + 1)
                    cols = slice(b * L, (b + 1) * L)
                    nc.vector.scalar_tensor_tensor(q_lo[:, cols], ps[:, 2 + b, :], bq_col[:, 0:1], q_hi[:, cols], ALU.add,
                                                   ALU.subtract).then_inc(operands_ready, 1)

            def low_keys(pair):
                for b in range(2):
                    dve.wait_ge(hi_ready, START + pair * 4 + 2 + b + 1)
                    nc.vector.scalar_tensor_tensor(k_lo[:, b, 0:L], ps[:, b, :], bks_col[:, 0:1], k_hi[:, b, 0:L], ALU.add, ALU.subtract)
                    nc.vector.scalar_tensor_tensor(k_lo[:, b, L:KEYS], ps[:, b, FAR * P:L], bk_far_col[:, 0:1], k_hi[:, b, L:KEYS],
                                                   ALU.add, ALU.subtract).then_inc(operands_ready, 1)

            def split_queries(pair):
                link = Links(dve_link, pair * SPLIT_LINKS)
                for b in range(2):
                    dve.wait_ge(proj_done, START + pair * 8 + 5 + b)
                    link(nc.vector.tensor_tensor(q_nat[:, b, :, :], ps[:, 2 + b, :].rearrange("p (l c) -> p l c", l=QT),
                                                 bq_row[:].unsqueeze(1).broadcast_to([P, QT, D]), ALU.add))
                    link.wait()
                    natural = q_nat[:, b, :, :].rearrange("p l (h d) -> p h l d", d=DK)
                    link(nc.vector.tensor_copy(q_split[:, b, :, 0, :, :], natural))
                    link.wait()
                    nc.vector.tensor_copy(q_split[:, b, :, 1, :, :], q_split[:, b, :, 0, :, :]).then_inc(q_split_ready, 1)
                    nc.vector.tensor_tensor(q_split[:, b, :, 2, :, :], natural, q_split[:, b, :, 0, :, :],
                                            ALU.subtract).then_inc(q_split_ready, 1)
                assert link.n == SPLIT_LINKS

            def values(pair):
                for b in range(2):
                    dve.wait_ge(proj_done, START + pair * 8 + 7 + b)
                    nc.vector.tensor_tensor(v_s[:, b * 4:b * 4 + 4, :], ps[:, 4 + b, :].rearrange("p (t c) -> p t c", t=RT),
                                            bv_row[:].unsqueeze(1).broadcast_to([P, RT, D]), ALU.add)
                    nc.vector.tensor_tensor(v_far[:, b, :, :], ps[:, 4 + b, FAR * P:L].rearrange("p (t c) -> p t c", t=RT - FAR),
                                            rv_last_row[:].unsqueeze(1).broadcast_to([P, RT - FAR, D]), ALU.add).then_inc(operands_ready, 1)

            def queries(pair, s, odd, first=False):
                if not first:
                    dve.wait_ge(score_done, START + pair * TILES + (s - 1) * QUADS)
                spread_queries(nc.vector, s, odd).then_inc(stat_ready, 1)

            def evacuate(pair, s, q):
                dve.wait_ge(tr_done, START + pair * TILES + s * QUADS + q + 1)
                nc.vector.tensor_copy(probs_t[:, q, :, :].rearrange("p r c -> p (r c)"), ps[:, 4 + q % 2, :]).then_inc(evac_dve, 1)

            def reciprocal(pair, s, q, first):
                dve.wait_ge(exp_done, START + pair * TILES + s * QUADS + q + 1)
                if not first:
                    dve.wait_ge(norm_done, START + pair * TILES + (s - 1) * QUADS + q + 1)
                nc.vector.reciprocal(inv_sum[:, q:q + 1], row_sum[:, q:q + 1]).then_inc(inv_done, 1)

            STEP_LINKS = 2

            def reduce_products(pair, s):
                link = Links(step_link, (pair * STEPS + s) * STEP_LINKS)
                dve.wait_ge(av_v_done, START + pair * STEPS + s + 1)
                link(nc.vector.tensor_tensor(v_masked[:], ps[:, 6, 0:256].rearrange("p (c h) -> p c h", h=4),
                                             m4.unsqueeze(1).broadcast_to([P, 2 * ROWS, 4]), ALU.mult))
                link.wait()
                for b in range(2):
                    last = nc.vector.tensor_reduce(attn_t[:, bass.ds(pair * TOK + b * L + s * ROWS, ROWS)],
                                                   v_masked[:, b * ROWS:(b + 1) * ROWS, :], op=ALU.add, axis=AX_X)
                last.then_inc(v_red, 1)
                dve.wait_ge(av_r_done, START + pair * STEPS + s + 1)
                link(nc.vector.tensor_tensor(r_masked[:], ps[:, 7, 0:256].rearrange("p (g l h) -> p g l h", l=QT, h=DK),
                                             m4.unsqueeze(1).unsqueeze(3).broadcast_to([P, 8, QT, DK]), ALU.mult))
                link.wait()
                nc.vector.tensor_reduce(rel_o[:].rearrange("p a (g h) -> p (a g) h", h=DK), r_masked[:].rearrange("p g l h -> p g h l"),
                                        op=ALU.add, axis=AX_X).then_inc(r_red, 1)

            def step(pair, s, odd, first=False, more=True):
                for q in range(QUADS):
                    if not first and q + 1 in DVE_EVAC:
                        evacuate(pair, s - 1, q + 1)
                    dve.wait_ge(score_done, START + pair * TILES + s * QUADS + q + 1)
                    nc.vector.tensor_reduce(neg_max[:, q:q + 1], ps[:, q % S_BANKS, :], op=ALU.max, axis=AX_X,
                                            negate=True).then_inc(max_done, 1)
                    if q >= LAG:
                        reciprocal(pair, s, q - LAG, first)
                for q in range(QUADS - LAG, QUADS):
                    reciprocal(pair, s, q, first)
                if more:
                    queries(pair, s + 2, odd)

            def first_queries(pair):
                dve.wait_ge(q_twice_landed, START + (pair + 1) * 64)
                queries(pair, 0, 0, first=True)

            def last_step(pair, ahead):
                link = Links(ffn_link, 0)
                if not ahead:
                    prepare_attention(0, link)
                for q in DVE_EVAC[:1]:
                    evacuate(pair, STEPS - 1, q)
                if ahead:
                    low_queries(pair + 1)
                    low_keys(pair + 1)
                else:
                    prepare_residual(0, 0, link)
                for q in DVE_EVAC[1:]:
                    evacuate(pair, STEPS - 1, q)
                if ahead:
                    split_queries(pair + 1)
                    first_queries(pair + 1)
                else:
                    prepare_norm(0, 0, link)
                    low_weights(1, w2_s, w2_h, w2_l)
                    nc.vector.tensor_scalar(b2_s[:], b2_s[:], W_SCALE, None, ALU.mult).then_inc(w_low, 1)
                reduce_products(pair, STEPS - 1)
                if ahead:
                    values(pair + 1)
                else:
                    prepare_low(0, 0)
                    prepare_gates(0, link)
                    prepare_comb(0, 0, link)
                    assert link.n == FFN_LINKS, link.n

            def low_weights(n, weights, high, low):
                dve.wait_ge(w_high, n + 1)
                nc.vector.scalar_tensor_tensor(low[:], weights[:], W_SCALE, high[:], ALU.mult, ALU.subtract).then_inc(w_low, 1)

            def pair_steps(pair, ahead):
                step(pair, 0, 0, first=True)
                with dve.Fori(0, STEPS // 2 - 2) as i:
                    step(pair, 2 * i + 1, 1)
                    reduce_products(pair, 2 * i)
                    step(pair, 2 * i + 2, 0)
                    reduce_products(pair, 2 * i + 1)
                step(pair, STEPS - 3, 1)
                reduce_products(pair, STEPS - 4)
                step(pair, STEPS - 2, 0, more=False)
                reduce_products(pair, STEPS - 3)
                if ahead:
                    variances(pair + 1)
                step(pair, STEPS - 1, 1, more=False)
                if ahead:
                    normalised(pair + 1)
                else:
                    dve.wait_ge(ffn_loaded, 16 * FFN_LOADS)
                    low_weights(0, w1_s, w1_h, w1_l)
                reduce_products(pair, STEPS - 2)
                last_step(pair, ahead)

            FFN_LINKS = 12

            def prepare_attention(b, link):
                dve.wait_ge(rel_nat_tr, START + b + 1)
                nc.vector.tensor_tensor(o_sum_t, ps[:, 0, :], attn_t[:, bass.ds(b * L, L)], ALU.add).then_inc(o_ready, 1)

            def prepare_residual(b, slot, link):
                dve.wait_ge(wo_done, START + b + 1)
                rows = acc[:, slot, :, :]
                dve.wait_ge(x_batch_landed, START + (b + 1) * 16)
                link(nc.vector.tensor_tensor(xn[:, 0:TPB, :], ps[:, 1, :].rearrange("p (t d) -> p t d", t=TPB), x_batch, ALU.add))
                link.wait()
                link(nc.vector.tensor_tensor(rows, xn[:, 0:TPB, :], bo_row[:].unsqueeze(1).broadcast_to([P, TPB, D]), ALU.add))
                link.wait()
                for t in range(TPB):
                    last = nc.vector.bn_stats(stats[:, t, :], acc[:, slot, t, :])
                link(last)
                link.settle()
                for t in range(TPB):
                    last = nc.vector.bn_aggr(mv[:, t, :], stats[:, t, :])
                link(last)
                link.wait()
                nc.vector.tensor_scalar(var_eps[:, 0:TPB], mv[:, 0:TPB, 1], LN_EPS, None, ALU.add).then_inc(x1_var, 1)

            def prepare_norm(b, slot, link):
                dve.wait_ge(x1_rstd, START + b + 1)
                for t in range(TPB):
                    last = nc.vector.tensor_scalar(xn[:, t, :], acc[:, slot, t, :], mv[:, t, 0:1], rstd[:, t:t + 1],
                                                   ALU.subtract, ALU.mult)
                last.then_inc(hn_ready, 1)

            def prepare_low(b, slot):
                dve.wait_ge(h_ready, START + 2 * b + 2)
                nc.vector.tensor_tensor(h_lo[:, slot, :], ps[:, 0, :], h_hi[:, slot, :], ALU.subtract).then_inc(h_low, 1)

            def prepare_gates(b, link):
                dve.wait_ge(gate_done, START + b + 1)
                link(nc.vector.tensor_tensor(gates[:], ps[:, 2, 0:TPB * NE].rearrange("p (t e) -> p t e", t=TPB),
                                             rb_row[:].unsqueeze(1).broadcast_to([P, TPB, NE]), ALU.add))
                link.settle()
                for t in range(TPB):
                    last = nc.vector.max(top8[:, t, :], gates[:, t, :])
                link(last)
                link.settle()
                for t in range(TPB):
                    last = nc.vector.max_index(top_i[:, t, :], top8[:, t, :], gates[:, t, :])
                link(last)
                link.wait()
                link(nc.vector.tensor_copy(top_f[:], top_i[:, :, 0:2]))
                nc.vector.tensor_tensor(gap[:], top8[:, :, 1], top8[:, :, 0], ALU.subtract).then_inc(gap_ready, 1)

            def prepare_comb(b, slot, link):
                dve.wait_ge(e_gap_ready, START + b + 1)
                link(nc.vector.tensor_scalar(prob2[:, :, 1], e_gap[:], 1.0, W_SCALE, ALU.add, ALU.mult))
                link.wait()
                link(nc.vector.reciprocal(prob2[:, :, 0], prob2[:, :, 1]))
                link.wait()
                link(nc.vector.tensor_tensor(prob2[:, :, 1], prob2[:, :, 0], e_gap[:], ALU.mult))
                link.wait()
                for t in range(TPB):
                    for j in range(2):
                        last = nc.vector.tensor_scalar(pick[:, t, j, :], iota8, top_f[:, t, j:j + 1], prob2[:, t, j:j + 1],
                                                       ALU.is_equal, ALU.mult)
                link(last)
                link.wait()
                nc.vector.tensor_tensor(comb[:, slot, :, NS:], pick[:, :, 0, :], pick[:, :, 1, :], ALU.add).then_inc(comb_ready, 1)

            def second_biases(b, slot):
                dve.wait_ge(bias_done, START + b + 1)
                nc.vector.tensor_tensor(acc[:, slot, :, :], ps[:, 3, :].rearrange("p (t d) -> p t d", t=TPB),
                                        acc[:, slot, :, :], ALU.add).then_inc(bias_added, 1)
                dve.wait_ge(bias_added, START + b + 1)

            def expert(b, slot, e):
                dve.wait_ge(down_done, SLOTS + b * EXPERTS + e + 1)
                for t in range(TPB):
                    last = nc.vector.scalar_tensor_tensor(acc[:, slot, t, :], ps[:, 6 + e % 2, t * D:(t + 1) * D],
                                                          comb[:, slot, t, e:e + 1], acc[:, slot, t, :], ALU.mult, ALU.add)
                last.then_inc(final_ready if e == EXPERTS - 1 else y_used, 1)
                if e < EXPERTS - 1:
                    dve.wait_ge(y_used, START + b * (EXPERTS - 1) + e + 1)
                else:
                    dve.wait_ge(final_ready, START + b + 1)

            def batch(b, slot, ahead):
                link = Links(ffn_link, (b + 1) * FFN_LINKS)
                for e in range(EXPERTS):
                    expert(b, slot, e)
                    if ahead:
                        if e == 0:
                            prepare_attention(b + 1, link)
                        if e == 1:
                            dve.wait_ge(stored, START + (b + 1 - 1) * 16)
                            prepare_residual(b + 1, 1 - slot, link)
                        if e == 2:
                            prepare_norm(b + 1, 1 - slot, link)
                        if e == 4:
                            prepare_low(b + 1, 1 - slot)
                        if e == 5:
                            prepare_gates(b + 1, link)
                        if e == 7:
                            prepare_comb(b + 1, 1 - slot, link)
                    if e == 2:
                        second_biases(b, slot)
                assert not ahead or link.n == FFN_LINKS, link.n

            def setup():
                dve.wait_ge(loaded, 16 * LOADS)
                nc.vector.tensor_copy(mask16h[:], const[:, M16:M16 + H]).then_inc(setup_dve, 1)
                nc.vector.tensor_copy(mask8h[:], const[:, M8:M8 + DK]).then_inc(setup_dve, 1)
                nc.vector.tensor_copy(mask4h[:], m4.unsqueeze(2).broadcast_to([P, QT, DK])).then_inc(setup_dve, 1)
                nc.vector.tensor_copy(identh[:], ident).then_inc(setup_dve, 1)
                nc.vector.tensor_copy(rk_split[:], rk3).then_inc(setup_dve, 1)
                nc.vector.tensor_scalar(wk_s[:], wk_s[:], SCALE, None, ALU.mult).then_inc(setup_dve, 1)
                nc.vector.tensor_scalar(bks_col[:], bk_col[:], SCALE, None, ALU.mult).then_inc(setup_dve, 1)
                nc.vector.tensor_tensor(rv_last_row[:], rv_last_row[:], bv_row[:], ALU.add).then_inc(setup_dve, 1)
                dve.wait_ge(setup_dve, 8)
                nc.vector.tensor_tensor(bk_far_col[:], bks_col[:], rk_last_col[:], ALU.add).then_inc(setup_dve, 1)
                nc.vector.tensor_tensor(rk_split[32:64, :], rk3[32:64, :], rk_split[32:64, :], ALU.subtract).then_inc(setup_dve, 1)
                dve.wait_ge(setup_dve, SETUP_DVE)
                dve.wait_ge(setup_pool, SETUP_POOL)

            variances(0)
            normalised(0)
            setup()
            low_queries(0)
            low_keys(0)
            split_queries(0)
            first_queries(0)
            values(0)
            with dve.Fori(0, PAIRS - 1) as pair:
                pair_steps(pair, True)
            pair_steps(PAIRS - 1, False)
            with dve.Fori(0, B // 2 - 1) as i:
                batch(2 * i, 0, True)
                batch(2 * i + 1, 1, True)
            batch(B - 2, 0, True)
            batch(B - 1, 1, False)

        @block.tensor
        def _(pe):
            pe.wait_ge(loaded, 16 * LOADS)

            def rows_t(pair):
                for half in range(2):
                    pe.wait_ge(xn_ready, START + pair * 8 + half * 4 + 4)
                    for t in range(4):
                        last = nc.tensor.transpose(ps[:, half, t * P:(t + 1) * P], xn[:, half * 4 + t, :], ident)
                    last.then_inc(xn_tr, 1)

            def project(w, bank):
                for b in range(2):
                    nc.tensor.matmul(ps[:, bank + b, :], w[:], xn_t[:, b * L:(b + 1) * L], start=True, stop=True).then_inc(proj_done, 1)

            def project_queries(pair):
                pe.wait_ge(xn_t_ready, START + pair * 2 + 2)
                project(wq_s, 2)

            def project_keys(pair):
                project(wk_s, 0)

            def natural_queries(pair):
                pe.wait_ge(operands_ready, START + pair * 6 + 2)
                for b in range(2):
                    for l in range(QT):
                        rows = xn_t[:, b * L:(b + 1) * L].rearrange("p (q l) -> p l q", l=QT)[:, l, :]
                        last = nc.tensor.matmul(ps[:, 2 + b, l * D:(l + 1) * D], rows, wq_s[:], start=True, stop=True)
                    last.then_inc(proj_done, 1)

            def relative_queries(pair, b):
                if b == 0:
                    pe.wait_ge(operands_ready, START + pair * 6 + 4)
                pe.wait_ge(q_split_ready, START + pair * 4 + b * 2 + 2)
                for half in range(2):
                    for h in range(8):
                        pieces = q_split[:, b, half * 8 + h, :, :, :].rearrange("p a l d -> p (a l d)")
                        last = nc.tensor.transpose(bank_h(b * 2 + half, 8 * P)[0:REL_K, h * P:(h + 1) * P], pieces, identh[:])
                    last.then_inc(q_rel_tr, 1)

            def project_values(pair):
                for b in range(2):
                    for t in range(RT):
                        last = nc.tensor.matmul(ps[:, 4 + b, t * D:(t + 1) * D], xn_t[:, b * L + t * P:b * L + (t + 1) * P], wv_s[:],
                                                start=True, stop=True)
                    last.then_inc(proj_done, 1)

            def operands(pair):
                pe.wait_ge(q_rel_ready, START + pair * 4 + 4)
                pe.wait_ge(k_both_landed, START + (pair + 1) * 64)

            def scores(pair, s, q, odd, group, first, first_odd):
                if q == 0:
                    if odd and first_odd:
                        pe.wait_ge(stat_first_odd, START + pair + 1)
                    else:
                        pe.wait_ge(stat_ready, START + pair * (STEPS - 1) + s + (1 if first else 0))
                    pe.wait_ge(stat_rel_ready, START + pair * STEPS + s + 1)
                    pe.wait_ge(rk_landed[odd], START + (pair * STEPS + s - odd + 2) * 8)
                if not (first and q < S_BANKS):
                    pe.wait_ge(exp_done, START + pair * TILES + s * QUADS + q - S_BANKS + 1)

                def keys(b):
                    return b.rearrange("k (a c) -> k a c", c=FAR * P)[:, 0::2, :] if group == 0 else b[:, 0:L]

                def columns(b):
                    return b.rearrange("p (a c) -> p a c", c=FAR * P) if group == 0 else b

                for b in range(2):
                    for half in range(2):
                        at = b * 64 + half * 32
                        nc.tensor.matmul(columns(ps[at:at + 32, q % S_BANKS, :]), stat_hi[odd][:, half, b, q, :], keys(k_both[:, half, b, :]),
                                         start=True, stop=False, skip_group_check=True)
                for b in range(2):
                    nc.tensor.matmul(columns(ps[b * 64:b * 64 + 64, q % S_BANKS, :]), stat_lo[odd][:, b, q, :, :].rearrange("p a c -> p (a c)"),
                                     keys(k_hi[:, b, :]), start=False, stop=False, skip_group_check=True)
                near = FAR * P if group == 0 else L
                window = (ROWS - QT) - QT * q
                nc.tensor.matmul(ps[:, q % S_BANKS, 0:near], stat_rel[odd][:, q, :, :, :].rearrange("k g l h -> k (g l h)"),
                                 rk_step[:, odd, window:window + near], start=False, stop=True, skip_group_check=True).then_inc(score_done, 1)

            def transposes(pair, s, q):
                pe.wait_ge(norm_done, START + pair * TILES + s * QUADS + q + 1)
                if q >= 2:
                    if q - 2 in ACT_EVAC:
                        pe.wait_ge(evac_act, START + (pair * STEPS + s) * len(ACT_EVAC) + ACT_EVAC.index(q - 2) + 1)
                    else:
                        pe.wait_ge(evac_dve, START + (pair * STEPS + s) * len(DVE_EVAC) + DVE_EVAC.index(q - 2) + 1)
                for rt in range(RT):
                    last = nc.tensor.transpose(ps[:, 4 + q % 2, rt * P:(rt + 1) * P], probs[:, q, rt * P:(rt + 1) * P], ident)
                last.then_inc(tr_done, 1)

            def value_products(pair, s, group):
                pe.wait_ge(evac_act, START + (pair * STEPS + s + 1) * len(ACT_EVAC))
                pe.wait_ge(evac_dve, START + (pair * STEPS + s + 1) * len(DVE_EVAC))
                pe.wait_ge(v_red, START + pair * STEPS + s)
                pe.wait_ge(rel_t_ready, START + pair * STEPS + s)
                for b in range(2):
                    for rt in range(RT):
                        for g in range(4):
                            at = b * 64 + (g // 2) * 32
                            cols = probs_t[:, :, rt, at:at + 32].rearrange("p q (l h) -> p q l h", l=QT)[:, :, :, (g % 2) * 4:(g % 2) * 4 + 4]
                            values = v_s[:, b * 4 + rt, :] if rt < group + FAR else v_far[:, b, rt - FAR, :]
                            last = nc.tensor.matmul(ps[32 * g:32 * g + 32, 6, b * P:(b + 1) * P], values[:, 32 * g:32 * g + 32], cols,
                                                    start=rt == 0, stop=rt == RT - 1, skip_group_check=True)
                last.then_inc(av_v_done, 1)

            def relative_products(pair, s, group):
                pe.wait_ge(rv_landed, START + (pair * STEPS + s + 1) * 16)
                pe.wait_ge(r_red, START + pair * STEPS + s)
                near = min(RT, group + FAR)
                for half in range(2):
                    for rt in range(near):
                        for g in range(4):
                            q = half * 4 + g
                            last = nc.tensor.matmul(ps[32 * g:32 * g + 32, 7, half * P:(half + 1) * P], rv_step[:, RT - 1 - rt, q * 32:q * 32 + 32],
                                                    probs_t[:, q, rt, :], start=rt == 0, stop=rt == near - 1, skip_group_check=True)
                last.then_inc(av_r_done, 1)

            def rel_transposes(pair, s):
                pe.wait_ge(r_red, START + pair * STEPS + s + 1)
                pe.wait_ge(v_red, START + pair * STEPS + s + 1)
                for half in range(2):
                    last = nc.tensor.transpose(ps[0:32, 6, 256 + half * P:256 + (half + 1) * P], rel_o[:, half, :], ident)
                last.then_inc(rel_tr, 1)

            def step(pair, s, odd, group, before, first=False, rel=True):
                if not first:
                    transposes(pair, s - 1, 0)
                for q in range(QUADS):
                    if not first and q + 1 < QUADS:
                        transposes(pair, s - 1, q + 1)
                    if rel and q == 4:
                        rel_transposes(pair, s - 2)
                    scores(pair, s, q, odd, group, first, not rel)
                if not first:
                    value_products(pair, s - 1, before)
                    relative_products(pair, s - 1, before)

            def last_step(pair, ahead):
                s = STEPS - 1
                for q in range(QUADS):
                    transposes(pair, s, q)
                    if q == 4:
                        rel_transposes(pair, s - 1)
                    if q == 1:
                        pe.wait_ge(exp_done, START + (pair + 1) * TILES)
                    if ahead:
                        if q == 1:
                            rows_t(pair + 1)
                        if q == 3:
                            project_queries(pair + 1)
                        if q == 5:
                            project_keys(pair + 1)
                    else:
                        if q == 1:
                            prepare_attention(0)
                        if q == 4:
                            pe.wait_ge(ffn_loaded, 16 * FFN_LOADS)
                            prepare_output(0)
                        if q == 7:
                            prepare_h(0)
                if ahead:
                    natural_queries(pair + 1)
                value_products(pair, s, GROUPS - 1)
                if ahead:
                    relative_queries(pair + 1, 0)
                else:
                    prepare_gates(0, 0)
                relative_products(pair, s, GROUPS - 1)
                if ahead:
                    relative_queries(pair + 1, 1)
                    project_values(pair + 1)
                rel_transposes(pair, s)
                if ahead:
                    operands(pair + 1)

            def pair_steps(pair, ahead):
                step(pair, 0, 0, 0, 0, first=True, rel=False)
                pe.wait_ge(operands_ready, START + pair * 6 + 6)
                for s in range(1, NEAR_GROUP * GROUP_STEPS + 1):
                    step(pair, s, s % 2, s // GROUP_STEPS, (s - 1) // GROUP_STEPS, rel=s > 1)
                with pe.Fori(NEAR_GROUP * GROUP_STEPS // 2, STEPS // 2 - 1) as i:
                    step(pair, 2 * i + 1, 1, GROUPS - 1, GROUPS - 1)
                    step(pair, 2 * i + 2, 0, GROUPS - 1, GROUPS - 1)
                step(pair, STEPS - 1, 1, GROUPS - 1, GROUPS - 1)
                last_step(pair, ahead)

            def prepare_attention(b):
                pe.wait_ge(rel_landed, START + (b + 1) * 16 * TPB)
                for t in range(TPB):
                    last = nc.tensor.transpose(ps[:, 0, t * P:(t + 1) * P], rel_nat[:, t, :, :].rearrange("p h d -> p (h d)"), ident)
                last.then_inc(rel_nat_tr, 1)

            def prepare_output(b):
                pe.wait_ge(o_ready, START + b + 1)
                for t in range(TPB):
                    last = nc.tensor.matmul(ps[:, 1, t * D:(t + 1) * D], o_sum_t[:, t * P:(t + 1) * P], wo_s[:], start=True, stop=True)
                last.then_inc(wo_done, 1)

            def prepare_h(b):
                pe.wait_ge(hn_ready, START + b + 1)
                for t in range(TPB):
                    last = nc.tensor.transpose(ps[:, 0, t * P:(t + 1) * P], xn[:, t, :], ident)
                last.then_inc(hn_tr, 1)

            def prepare_gates(b, slot):
                pe.wait_ge(h_ready, START + 2 * b + 1)
                for t in range(TPB):
                    last = nc.tensor.matmul(ps[:, 2, t * NE:(t + 1) * NE], h_t[:, slot, t * P:(t + 1) * P], rw_s[:], start=True, stop=True)
                last.then_inc(gate_done, 1)

            def prepare_comb(b, slot):
                pe.wait_ge(comb_ready, START + b + 1)
                for t in range(TPB):
                    last = nc.tensor.transpose(ps[0:EXPERTS, 2, t * P:(t + 1) * P], comb[:, slot, t, :], ident)
                last.then_inc(comb_tr, 1)

            def second_biases(b):
                pe.wait_ge(comb_t_ready, START + b + 1)
                for t in range(TPB):
                    last = nc.tensor.matmul(ps[:, 3, t * D:(t + 1) * D], comb_t[:, t * P:(t + 1) * P], b2_s[:], start=True, stop=True)
                last.then_inc(bias_done, 1)

            def up(b, slot, e):
                if e == 0:
                    pe.wait_ge(h_low, START + b + 1)
                for k in range(2):
                    pe.wait_ge(gelu_done, START + b * 20 + (e * 2 + k - 1 if e else 0))
                    cols = slice(k * P, (k + 1) * P)
                    nc.tensor.matmul(ps[:, 4 + k, :], w1_h[:, e, cols], h_hi[:, slot, :], start=True, stop=False)
                    nc.tensor.matmul(ps[:, 4 + k, :], w1_h[:, e, cols], h_lo[:, slot, :], start=False, stop=False)
                    nc.tensor.matmul(ps[:, 4 + k, :], w1_l[:, e, cols], h_hi[:, slot, :], start=False, stop=True).then_inc(up_done, 1)

            def down(b, slot, e):
                pe.wait_ge(hid_low, SLOTS + b * EXPERTS + e + 1)
                if e >= 2:
                    pe.wait_ge(y_used, START + b * (EXPERTS - 1) + e - 1)
                else:
                    pe.wait_ge(final_ready, START + b)
                place = (slot * EXPERTS + e) % SLOTS
                for t in range(TPB):
                    for k in range(2):
                        rows = slice(t * P, (t + 1) * P)
                        y = ps[:, 6 + e % 2, t * D:(t + 1) * D]
                        nc.tensor.matmul(y, hid_h[:, place, k, rows], w2_h[:, e, k, :], start=k == 0, stop=False)
                        nc.tensor.matmul(y, hid_h[:, place, k, rows], w2_l[:, e, k, :], start=False, stop=False)
                        last = nc.tensor.matmul(y, hid_l[:, place, k, rows], w2_h[:, e, k, :], start=False, stop=k == 1)
                last.then_inc(down_done, 1)

            def batch(b, slot, ahead):
                for e in range(EXPERTS):
                    if e + LOOK < EXPERTS:
                        up(b, slot, e + LOOK)
                    elif ahead:
                        up(b + 1, 1 - slot, e + LOOK - EXPERTS)
                    down(b, slot, e)
                    if ahead:
                        if e == 0:
                            prepare_attention(b + 1)
                        if e == 1:
                            prepare_output(b + 1)
                        if e == 4:
                            prepare_h(b + 1)
                        if e == 5:
                            prepare_gates(b + 1, 1 - slot)
                        if e == 9:
                            prepare_comb(b + 1, 1 - slot)
                    if e == 1:
                        second_biases(b)

            rows_t(0)
            pe.wait_ge(setup_dve, SETUP_DVE)
            project_queries(0)
            project_keys(0)
            natural_queries(0)
            project_values(0)
            for b in range(2):
                relative_queries(0, b)
            operands(0)
            with pe.Fori(0, PAIRS - 1) as pair:
                pair_steps(pair, True)
            pair_steps(PAIRS - 1, False)
            pe.wait_ge(rel_t_ready, START + PAIRS * STEPS)
            pe.wait_ge(w_low, 3)
            for e in range(LOOK):
                up(0, 0, e)
            prepare_comb(0, 0)
            with pe.Fori(0, B // 2 - 1) as i:
                batch(2 * i, 0, True)
                batch(2 * i + 1, 1, True)
            batch(B - 2, 0, True)
            batch(B - 1, 1, False)


def relative_windows(table_k, table_v):
    n = 2 * MAX_LEN - 1

    def at(apart):
        index = apart + MAX_LEN - 1
        return np.clip(np.where(index < 0, index + n, index), 0, n - 1)

    rows, cols = np.arange(QT)[:, None], np.arange(RK_COLS)[None, :]
    keys = table_k[at(cols - (L - QT) - rows)]
    rk = np.ascontiguousarray(keys.transpose(0, 2, 1).reshape(QT * DK, RK_COLS))
    part, cols = np.arange(P)[:, None], np.arange(RV_COLS)[None, :]
    rv = np.ascontiguousarray(table_v[at(part - cols + (L - P))].reshape(P, RV_COLS * DK))
    return rk, rv


def constants():
    row = np.arange(P)[:, None]
    c = np.zeros((P, CONSTS), np.float32)
    c[:, M4:M4 + 4] = (row // DK) % 4 == np.arange(4)[None, :]
    c[:, M16:M16 + H] = row // DK == np.arange(H)[None, :]
    c[:, IOTA:IOTA + NE] = np.arange(NE)[None, :]
    c[:, M8:M8 + DK] = (row // DK) % 8 == np.arange(DK)[None, :]
    c[:, IDENT:] = np.eye(P)
    return c


def kernel(**inputs):
    import concourse.bacc as bacc
    from concourse.bass_utils import run_bass_kernel_spmd

    given = {name: np.asarray(a) for name, a in inputs.items()}
    rk, rv = relative_windows(given["L0_attn_relative_k"], given["L0_attn_relative_v"])
    arrays = {"x": given["L0_attn_x"].reshape(B * L, D)}
    arrays["w_qkv"] = np.stack([given["L0_attn_" + name].T for name in ("Wq", "Wk", "Wv")], 1)
    last_k, last_v = (np.tile(given["L0_attn_relative_" + name][2 * MAX_LEN - 2], H) for name in ("k", "v"))
    arrays["cols"] = np.stack([given["L0_attn_bq"], given["L0_attn_bk"], last_k], 1)
    arrays["rows"] = np.concatenate([given["L0_attn_bq"], given["L0_attn_bv"], last_v])
    arrays |= {"wo_t": given["L0_attn_Wo"].T, "bo": given["L0_attn_bo"], "rk_win": np.concatenate([rk] * 3), "rv_win": rv}
    for name, short in (("router_w", "rw"), ("router_b", "rb"), ("w1", "w1"), ("w2", "w2"), ("b2", "b2"),
                        ("sw1", "sw1"), ("sw2", "sw2"), ("sb2", "sb2")):
        arrays[short] = given["L0_ffn_" + name]
    b1 = np.concatenate([given["L0_ffn_sb1"], given["L0_ffn_b1"]])
    arrays["b1_cols"] = b1.reshape(EXPERTS, 2, P).transpose(2, 0, 1)
    arrays["consts"] = constants()

    nc = bacc.Bacc("TRN2", target_bir_lowering=False, num_devices=1)
    args, in_map = [], {}
    for name, a in arrays.items():
        a = np.ascontiguousarray(a)
        in_map["in_" + name] = a
        args.append(nc.dram_tensor("in_" + name, a.shape, mybir.dt.from_np(a.dtype), kind="ExternalInput").ap())
    args.append(nc.dram_tensor("rel_scratch", (B * H, L * DK), F32, kind="Internal").ap())
    args.append(nc.dram_tensor("out", (B * L, D), F32, kind="ExternalOutput").ap())
    attention_ffn(nc, *args)
    r = run_bass_kernel_spmd(nc, [in_map], core_ids=[0])
    return r.results[0]["out"].reshape(B, L, D)
```
